# Optimizing a Trainium2 kernel written in Bass

```python
import numpy as np
import jax
import jax.numpy as jnp

def _softmax(x, axis=-1):
    return jax.nn.softmax(x, axis=axis)

def _gelu(x):
    return jax.nn.gelu(x, approximate=True)

def _silu(x):
    return jax.nn.silu(x)

def _sigmoid(x):
    return jax.nn.sigmoid(x)

def _layernorm(x, axis=-1, eps=1e-05):
    m = jnp.mean(x, axis=axis, keepdims=True)
    v = jnp.var(x, axis=axis, keepdims=True)
    return (x - m) / jnp.sqrt(v + eps)

def _scatter_add(tgt, idx, src, axis=0):
    return tgt.at[idx].add(src)

def _segment_sum(src, seg, n):
    return jax.ops.segment_sum(src, seg, n)
kernel_name = 'mk_xattn_seq_d2_seqx_r4_7c990b'

def setup_inputs(seed: int=0):
    np.random.seed(seed)
    _w = jnp.asarray

    def _rec_inputs():
        import jax
        import jax.numpy as jnp
        _rk = jax.random.key(seed)
        x = -0.000125 + 0.9999 * jax.random.normal(jax.random.fold_in(_rk, 1), (8, 256, 512), jnp.float32)
        _lenS = 256 - jax.random.randint(jax.random.fold_in(_rk, 7), (8,), 0, max(1, 256 // 4) + 1, jnp.int32)
        _lenS2 = 256 - jax.random.randint(jax.random.fold_in(_rk, 8), (8,), 0, max(1, 256 // 4) + 1, jnp.int32)
        _ctx_2048P = jax.random.normal(jax.random.fold_in(_rk, 11), (8, 16, 512), jnp.float32)
        _ctx_2048c = jax.random.dirichlet(jax.random.fold_in(_rk, 511), 0.3 * jnp.ones((16,), jnp.float32), (8, 256))
        _ctx_2048t = jnp.einsum('bsk,bkd->bsd', _ctx_2048c, _ctx_2048P)
        _ctx_2048t = _ctx_2048t * jax.lax.rsqrt(jnp.mean(jnp.square(_ctx_2048t)) + 1e-12) * 0.953939
        ctx_2048 = -1.52775e-05 + 0.999936 * (_ctx_2048t + 0.3 * jax.random.normal(jax.random.fold_in(_rk, 611), (8, 256, 512), jnp.float32))
        return (x, ctx_2048)
    x, ctx_2048 = _rec_inputs()

    def _L0_xattn_setup():
        import jax, jax.numpy as jnp
        import numpy as np
        B, C, CI, N = (16, 256, 128, 512)
        EPS = 1e-05

        def _conv1x1(w, b, x):
            return jnp.einsum('oc,bcn->bon', w, x) + b[None, :, None]
        key = jax.random.key(seed)
        ks = jax.random.split(key, 14)
        s = 0.02
        return {'x': jax.random.normal(ks[0], (B, C, N), jnp.float32), 'x_2': jax.random.normal(ks[1], (B, C, N), jnp.float32), 'theta_w': jax.random.normal(ks[2], (CI, C), jnp.float32) * s, 'theta_b': jax.random.normal(ks[3], (CI,), jnp.float32) * s, 'phi_w': jax.random.normal(ks[4], (CI, C), jnp.float32) * s, 'phi_b': jax.random.normal(ks[5], (CI,), jnp.float32) * s, 'g_w': jax.random.normal(ks[6], (CI, C), jnp.float32) * s, 'g_b': jax.random.normal(ks[7], (CI,), jnp.float32) * s, 'w_w': jax.random.normal(ks[8], (C, CI), jnp.float32) * s, 'w_b': jax.random.normal(ks[9], (C,), jnp.float32) * s, 'bn_gamma': jax.random.normal(ks[10], (C,), jnp.float32), 'bn_beta': jax.random.normal(ks[11], (C,), jnp.float32), 'bn_mean': jax.random.normal(ks[12], (C,), jnp.float32), 'bn_var': jax.random.uniform(ks[13], (C,), jnp.float32, 0.5, 1.5)}
    _L0_xattn_all = _L0_xattn_setup()
    _L0_xattn_in = {k: v for k, v in _L0_xattn_all.items() if k in ('theta_w', 'theta_b', 'phi_w', 'phi_b', 'g_w', 'g_b', 'w_w', 'w_b', 'bn_gamma', 'bn_beta', 'bn_mean', 'bn_var')}
    del _L0_xattn_all

    def _L1_xattn_setup():
        import jax, jax.numpy as jnp
        import numpy as np
        B, Q, S1, S2 = (4, 64, 512, 512)
        D, H, K, F = (512, 16, 128, 2048)
        LN_EPS = 1e-05

        def _layer_norm(x, scale, offset):
            mu = jnp.mean(x, axis=-1, keepdims=True)
            var = jnp.var(x, axis=-1, keepdims=True)
            return (x - mu) * jax.lax.rsqrt(var + LN_EPS) * scale + offset

        def _cross_attention(q_in, kv_in, wq, bq, wk, bk, wv, bv, wo, bo, bias_k, bias_v):
            b, q_len, _ = q_in.shape
            t = kv_in.shape[1]
            qh = (q_in @ wq + bq).reshape(b, q_len, H, K)
            kh = (kv_in @ wk + bk).reshape(b, t, H, K)
            vh = (kv_in @ wv + bv).reshape(b, t, H, K)
            kh = jnp.concatenate([kh, jnp.broadcast_to(bias_k, (b, 1, H, K))], axis=1)
            vh = jnp.concatenate([vh, jnp.broadcast_to(bias_v, (b, 1, H, K))], axis=1)
            scale = jnp.sqrt(jnp.asarray(K, q_in.dtype))
            logits = jnp.einsum('bqhk,bthk->bhqt', qh, kh) / scale
            weights = jax.nn.softmax(logits, axis=-1)
            ctx = jnp.einsum('bhqt,bthk->bqhk', weights, vh).reshape(b, q_len, H * K)
            return ctx @ wo + bo

        def _forward(x, xf_1, xf_2, ln1_scale, ln1_offset, wq1, bq1, wk1, bk1, wv1, bv1, wo1, bo1, bias_k1, bias_v1, ln2_scale, ln2_offset, wq2, bq2, wk2, bk2, wv2, bv2, wo2, bo2, bias_k2, bias_v2, ln_mlp_scale, ln_mlp_offset, w_fc1, b_fc1, w_fc2, b_fc2):
            res = x
            h = _layer_norm(x, ln1_scale, ln1_offset)
            x = res + _cross_attention(h, xf_1, wq1, bq1, wk1, bk1, wv1, bv1, wo1, bo1, bias_k1, bias_v1)
            res = x
            h = _layer_norm(x, ln2_scale, ln2_offset)
            x = res + _cross_attention(h, xf_2, wq2, bq2, wk2, bk2, wv2, bv2, wo2, bo2, bias_k2, bias_v2)
            h = _layer_norm(x, ln_mlp_scale, ln_mlp_offset)
            h = jax.nn.gelu(h @ w_fc1 + b_fc1, approximate=False) @ w_fc2 + b_fc2
            return x + h
        key = jax.random.key(seed)
        ks = iter(jax.random.split(key, 64))

        def rn(shape, s=0.02):
            return jax.random.normal(next(ks), shape, jnp.float32) * s
        inp = {'x': rn((B, Q, D), 1.0), 'xf_1': rn((B, S1, D), 1.0), 'xf_2': rn((B, S2, D), 1.0)}
        for i in (1, 2):
            inp[f'ln{i}_scale'] = jnp.ones((D,), jnp.float32)
            inp[f'ln{i}_offset'] = jnp.zeros((D,), jnp.float32)
            inp[f'wq{i}'] = rn((D, H * K))
            inp[f'bq{i}'] = jnp.zeros((H * K,), jnp.float32)
            inp[f'wk{i}'] = rn((D, H * K))
            inp[f'bk{i}'] = jnp.zeros((H * K,), jnp.float32)
            inp[f'wv{i}'] = rn((D, H * K))
            inp[f'bv{i}'] = jnp.zeros((H * K,), jnp.float32)
            inp[f'wo{i}'] = rn((H * K, D))
            inp[f'bo{i}'] = jnp.zeros((D,), jnp.float32)
            inp[f'bias_k{i}'] = rn((1, 1, H, K))
            inp[f'bias_v{i}'] = rn((1, 1, H, K))
        inp['ln_mlp_scale'] = jnp.ones((D,), jnp.float32)
        inp['ln_mlp_offset'] = jnp.zeros((D,), jnp.float32)
        inp['w_fc1'] = rn((D, F))
        inp['b_fc1'] = jnp.zeros((F,), jnp.float32)
        inp['w_fc2'] = rn((F, D))
        inp['b_fc2'] = jnp.zeros((D,), jnp.float32)
        return inp
    _L1_xattn_all = _L1_xattn_setup()
    _L1_xattn_in = {k: v for k, v in _L1_xattn_all.items() if k in ('ln1_scale', 'ln1_offset', 'wq1', 'bq1', 'wk1', 'bk1', 'wv1', 'bv1', 'wo1', 'bo1', 'bias_k1', 'bias_v1', 'ln2_scale', 'ln2_offset', 'wq2', 'bq2', 'wk2', 'bk2', 'wv2', 'bv2', 'wo2', 'bo2', 'bias_k2', 'bias_v2', 'ln_mlp_scale', 'ln_mlp_offset', 'w_fc1', 'b_fc1', 'w_fc2', 'b_fc2')}
    del _L1_xattn_all
    return {'x': x, 'ctx_2048': ctx_2048, 'L0_xattn_theta_w': _L0_xattn_in['theta_w'], 'L0_xattn_theta_b': _L0_xattn_in['theta_b'], 'L0_xattn_phi_w': _L0_xattn_in['phi_w'], 'L0_xattn_phi_b': _L0_xattn_in['phi_b'], 'L0_xattn_g_w': _L0_xattn_in['g_w'], 'L0_xattn_g_b': _L0_xattn_in['g_b'], 'L0_xattn_w_w': _L0_xattn_in['w_w'], 'L0_xattn_w_b': _L0_xattn_in['w_b'], 'L0_xattn_bn_gamma': _L0_xattn_in['bn_gamma'], 'L0_xattn_bn_beta': _L0_xattn_in['bn_beta'], 'L0_xattn_bn_mean': _L0_xattn_in['bn_mean'], 'L0_xattn_bn_var': _L0_xattn_in['bn_var'], 'L1_xattn_ln1_scale': _L1_xattn_in['ln1_scale'], 'L1_xattn_ln1_offset': _L1_xattn_in['ln1_offset'], 'L1_xattn_wq1': _L1_xattn_in['wq1'], 'L1_xattn_bq1': _L1_xattn_in['bq1'], 'L1_xattn_wk1': _L1_xattn_in['wk1'], 'L1_xattn_bk1': _L1_xattn_in['bk1'], 'L1_xattn_wv1': _L1_xattn_in['wv1'], 'L1_xattn_bv1': _L1_xattn_in['bv1'], 'L1_xattn_wo1': _L1_xattn_in['wo1'], 'L1_xattn_bo1': _L1_xattn_in['bo1'], 'L1_xattn_bias_k1': _L1_xattn_in['bias_k1'], 'L1_xattn_bias_v1': _L1_xattn_in['bias_v1'], 'L1_xattn_ln2_scale': _L1_xattn_in['ln2_scale'], 'L1_xattn_ln2_offset': _L1_xattn_in['ln2_offset'], 'L1_xattn_wq2': _L1_xattn_in['wq2'], 'L1_xattn_bq2': _L1_xattn_in['bq2'], 'L1_xattn_wk2': _L1_xattn_in['wk2'], 'L1_xattn_bk2': _L1_xattn_in['bk2'], 'L1_xattn_wv2': _L1_xattn_in['wv2'], 'L1_xattn_bv2': _L1_xattn_in['bv2'], 'L1_xattn_wo2': _L1_xattn_in['wo2'], 'L1_xattn_bo2': _L1_xattn_in['bo2'], 'L1_xattn_bias_k2': _L1_xattn_in['bias_k2'], 'L1_xattn_bias_v2': _L1_xattn_in['bias_v2'], 'L1_xattn_ln_mlp_scale': _L1_xattn_in['ln_mlp_scale'], 'L1_xattn_ln_mlp_offset': _L1_xattn_in['ln_mlp_offset'], 'L1_xattn_w_fc1': _L1_xattn_in['w_fc1'], 'L1_xattn_b_fc1': _L1_xattn_in['b_fc1'], 'L1_xattn_w_fc2': _L1_xattn_in['w_fc2'], 'L1_xattn_b_fc2': _L1_xattn_in['b_fc2']}

def reference(x, ctx_2048, L0_xattn_theta_w, L0_xattn_theta_b, L0_xattn_phi_w, L0_xattn_phi_b, L0_xattn_g_w, L0_xattn_g_b, L0_xattn_w_w, L0_xattn_w_b, L0_xattn_bn_gamma, L0_xattn_bn_beta, L0_xattn_bn_mean, L0_xattn_bn_var, L1_xattn_ln1_scale, L1_xattn_ln1_offset, L1_xattn_wq1, L1_xattn_bq1, L1_xattn_wk1, L1_xattn_bk1, L1_xattn_wv1, L1_xattn_bv1, L1_xattn_wo1, L1_xattn_bo1, L1_xattn_bias_k1, L1_xattn_bias_v1, L1_xattn_ln2_scale, L1_xattn_ln2_offset, L1_xattn_wq2, L1_xattn_bq2, L1_xattn_wk2, L1_xattn_bk2, L1_xattn_wv2, L1_xattn_bv2, L1_xattn_wo2, L1_xattn_bo2, L1_xattn_bias_k2, L1_xattn_bias_v2, L1_xattn_ln_mlp_scale, L1_xattn_ln_mlp_offset, L1_xattn_w_fc1, L1_xattn_b_fc1, L1_xattn_w_fc2, L1_xattn_b_fc2):
    import jax
    import jax.numpy as jnp

    def _L0_xattn_ref(x, x_2, theta_w, theta_b, phi_w, phi_b, g_w, g_b, w_w, w_b, bn_gamma, bn_beta, bn_mean, bn_var):
        import jax, jax.numpy as jnp
        import numpy as np
        B, C, CI, N = (16, 256, 128, 512)
        EPS = 1e-05

        def _conv1x1(w, b, x):
            return jnp.einsum('oc,bcn->bon', w, x) + b[None, :, None]
        g_x = _conv1x1(g_w, g_b, x_2).transpose(0, 2, 1)
        theta_x = _conv1x1(theta_w, theta_b, x).transpose(0, 2, 1)
        phi_x = _conv1x1(phi_w, phi_b, x_2)
        W = jnp.einsum('bnc,bcm->bnm', theta_x, phi_x) / phi_x.shape[-1]
        y = jnp.einsum('bnm,bmc->bnc', W, g_x).transpose(0, 2, 1)
        wy = _conv1x1(w_w, w_b, y)
        inv_std = jax.lax.rsqrt(bn_var + EPS)
        wy = bn_gamma[None, :, None] * (wy - bn_mean[None, :, None]) * inv_std[None, :, None] + bn_beta[None, :, None]
        return wy + x

    def _L1_xattn_ref(x, xf_1, xf_2, ln1_scale, ln1_offset, wq1, bq1, wk1, bk1, wv1, bv1, wo1, bo1, bias_k1, bias_v1, ln2_scale, ln2_offset, wq2, bq2, wk2, bk2, wv2, bv2, wo2, bo2, bias_k2, bias_v2, ln_mlp_scale, ln_mlp_offset, w_fc1, b_fc1, w_fc2, b_fc2):
        import jax, jax.numpy as jnp
        import numpy as np
        B, Q, S1, S2 = (4, 64, 512, 512)
        D, H, K, F = (512, 16, 128, 2048)
        LN_EPS = 1e-05

        def _layer_norm(x, scale, offset):
            mu = jnp.mean(x, axis=-1, keepdims=True)
            var = jnp.var(x, axis=-1, keepdims=True)
            return (x - mu) * jax.lax.rsqrt(var + LN_EPS) * scale + offset

        def _cross_attention(q_in, kv_in, wq, bq, wk, bk, wv, bv, wo, bo, bias_k, bias_v):
            b, q_len, _ = q_in.shape
            t = kv_in.shape[1]
            qh = (q_in @ wq + bq).reshape(b, q_len, H, K)
            kh = (kv_in @ wk + bk).reshape(b, t, H, K)
            vh = (kv_in @ wv + bv).reshape(b, t, H, K)
            kh = jnp.concatenate([kh, jnp.broadcast_to(bias_k, (b, 1, H, K))], axis=1)
            vh = jnp.concatenate([vh, jnp.broadcast_to(bias_v, (b, 1, H, K))], axis=1)
            scale = jnp.sqrt(jnp.asarray(K, q_in.dtype))
            logits = jnp.einsum('bqhk,bthk->bhqt', qh, kh) / scale
            weights = jax.nn.softmax(logits, axis=-1)
            ctx = jnp.einsum('bhqt,bthk->bqhk', weights, vh).reshape(b, q_len, H * K)
            return ctx @ wo + bo

        def _forward(x, xf_1, xf_2, ln1_scale, ln1_offset, wq1, bq1, wk1, bk1, wv1, bv1, wo1, bo1, bias_k1, bias_v1, ln2_scale, ln2_offset, wq2, bq2, wk2, bk2, wv2, bv2, wo2, bo2, bias_k2, bias_v2, ln_mlp_scale, ln_mlp_offset, w_fc1, b_fc1, w_fc2, b_fc2):
            res = x
            h = _layer_norm(x, ln1_scale, ln1_offset)
            x = res + _cross_attention(h, xf_1, wq1, bq1, wk1, bk1, wv1, bv1, wo1, bo1, bias_k1, bias_v1)
            res = x
            h = _layer_norm(x, ln2_scale, ln2_offset)
            x = res + _cross_attention(h, xf_2, wq2, bq2, wk2, bk2, wv2, bv2, wo2, bo2, bias_k2, bias_v2)
            h = _layer_norm(x, ln_mlp_scale, ln_mlp_offset)
            h = jax.nn.gelu(h @ w_fc1 + b_fc1, approximate=False) @ w_fc2 + b_fc2
            return x + h
        return _forward(x, xf_1, xf_2, ln1_scale, ln1_offset, wq1, bq1, wk1, bk1, wv1, bv1, wo1, bo1, bias_k1, bias_v1, ln2_scale, ln2_offset, wq2, bq2, wk2, bk2, wv2, bv2, wo2, bo2, bias_k2, bias_v2, ln_mlp_scale, ln_mlp_offset, w_fc1, b_fc1, w_fc2, b_fc2)
    x = _L0_xattn_ref(x, ctx_2048, L0_xattn_theta_w, L0_xattn_theta_b, L0_xattn_phi_w, L0_xattn_phi_b, L0_xattn_g_w, L0_xattn_g_b, L0_xattn_w_w, L0_xattn_w_b, L0_xattn_bn_gamma, L0_xattn_bn_beta, L0_xattn_bn_mean, L0_xattn_bn_var)
    x = _L1_xattn_ref(x, ctx_2048, ctx_2048, L1_xattn_ln1_scale, L1_xattn_ln1_offset, L1_xattn_wq1, L1_xattn_bq1, L1_xattn_wk1, L1_xattn_bk1, L1_xattn_wv1, L1_xattn_bv1, L1_xattn_wo1, L1_xattn_bo1, L1_xattn_bias_k1, L1_xattn_bias_v1, L1_xattn_ln2_scale, L1_xattn_ln2_offset, L1_xattn_wq2, L1_xattn_bq2, L1_xattn_wk2, L1_xattn_bk2, L1_xattn_wv2, L1_xattn_bv2, L1_xattn_wo2, L1_xattn_bo2, L1_xattn_bias_k2, L1_xattn_bias_v2, L1_xattn_ln_mlp_scale, L1_xattn_ln_mlp_offset, L1_xattn_w_fc1, L1_xattn_b_fc1, L1_xattn_w_fc2, L1_xattn_b_fc2)
    return x

_drawn_inputs = setup_inputs


def setup_inputs(seed=0):
    import zlib

    import numpy as np

    out = dict(_drawn_inputs(seed))
    spreads = {'L1_xattn_ln1_scale': (1.0, 0.6),
     'L1_xattn_ln1_offset': (0.0, 0.8),
     'L1_xattn_bq1': (0.0, 0.8),
     'L1_xattn_bk1': (0.0, 2.0),
     'L1_xattn_bv1': (0.0, 0.36),
     'L1_xattn_bo1': (0.0, 0.312),
     'L1_xattn_ln2_scale': (1.0, 0.6),
     'L1_xattn_ln2_offset': (0.0, 0.8),
     'L1_xattn_bq2': (0.0, 0.8),
     'L1_xattn_bk2': (0.0, 2.0),
     'L1_xattn_bv2': (0.0, 0.394),
     'L1_xattn_bo2': (0.0, 0.365),
     'L1_xattn_ln_mlp_scale': (1.0, 0.6),
     'L1_xattn_ln_mlp_offset': (0.0, 0.579),
     'L1_xattn_b_fc1': (0.0, 0.279),
     'L1_xattn_b_fc2': (0.0, 0.345)}
    factors = {'L0_xattn_theta_w': 3.481,
     'L0_xattn_theta_b': 8.0,
     'L0_xattn_phi_w': 3.337,
     'L0_xattn_phi_b': 8.0,
     'L0_xattn_g_w': 3.532,
     'L0_xattn_g_b': 8.0,
     'L0_xattn_w_w': 3.275,
     'L0_xattn_w_b': 4.371,
     'L1_xattn_wq1': 6.414,
     'L1_xattn_wk1': 6.262,
     'L1_xattn_bias_k1': 64.0,
     'L1_xattn_bias_v1': 64.0,
     'L1_xattn_wq2': 6.411,
     'L1_xattn_wk2': 6.281,
     'L1_xattn_bias_k2': 64.0,
     'L1_xattn_bias_v2': 64.0}
    for name, (base, spread) in spreads.items():
        noise = np.random.default_rng([zlib.crc32(name.encode()), seed]).standard_normal(out[name].shape)
        drawn = base * np.exp(spread * noise) if base else spread * noise
        out[name] = jnp.asarray(drawn.astype(out[name].dtype))
    for name, factor in factors.items():
        out[name] = (out[name] * factor).astype(out[name].dtype)
    return out
```

```python
from contextlib import ExitStack

import numpy as np
import concourse.bass as bass
from concourse import mybir

F32 = mybir.dt.float32
F32R = mybir.dt.float32r
ALU = mybir.AluOpType
ACT = mybir.ActivationFunctionType
AX = mybir.AxisListType

B, TOK, D = 8, 256, 512
CI = 128
H, K, F = 16, 128, 2048
P = 128
EPS = 1e-5
HALVES = 2
HB = B // HALVES
TILES = HB * TOK // P
CH = D // P
LAYERS = 2
BODIES = H // 2
MBODIES = F // 256
HBODIES = LAYERS * BODIES
STREAM = HBODIES + MBODIES
SCALE = float(1.0 / np.sqrt(np.float32(K)))

Q00, Q01, K10, K11, V10, V11, Q10, Q11 = range(8)
WO0 = 8
KN0, KN1, VN0, VN1 = 12, 13, 14, 15
WO1 = 16
UNITS = 20
ITEMS = 8
RING = 4
MUNITS = 12
ZUNITS = 2 * CH + 7 * HB

CR4, CR2, CR1 = 4, 2, 1
TO_V, TO_A = ("cT", "pg"), ("th", "M", "y", "wy")

FILL = [(u, s) for u in (K10, K11, V10, V11, Q10, Q11) for s in (0, 1)]
FILL += [(WO0 + t, 1) for t in range(4)]
FILL += [(u, s) for u in (KN0, KN1, VN0, VN1) for s in (0, 1)]
assert len(FILL) == 3 * 8


def ended(j, late):
    return [u for u, s in (FILL[3 * j + 2:3 * j + 3] if late else FILL[3 * j:3 * j + 2]) if s == 1]


def item(j):
    return j // 4, (j % 4) // 2, j % 2


def l0_units():
    units = [("cT", p, c) for p in range(2) for c in range(CH)]
    units += [("pg", 0, 0), ("pg", 0, 1), ("th", 0, 0)]
    for b in range(HB):
        nxt = b + 1 < HB
        units.append(("M", b, 0))
        units += [("pg", b + 1, 0), ("pg", b + 1, 1)] if nxt else []
        units.append(("y", b, 0))
        units += [("th", b + 1, 0)] if nxt else []
        units += [("wy", b, 0), ("wy", b, 1)]
    return units


L0 = l0_units()
assert len(L0) == ZUNITS and ZUNITS % RING == 0


def l0_taken(c, by):
    return sum(u[0] in by for u in L0[:c + 1])


def l0_units():
    units = [("cT", p, c) for p in range(2) for c in range(CH)]
    units += [("pg", 0, 0), ("pg", 0, 1), ("th", 0, 0)]
    for b in range(HB):
        nxt = b + 1 < HB
        units.append(("M", b, 0))
        units += [("pg", b + 1, 0), ("pg", b + 1, 1)] if nxt else []
        units.append(("y", b, 0))
        units += [("th", b + 1, 0)] if nxt else []
        units += [("wy", b, 0), ("wy", b, 1)]
    return units


L0 = l0_units()
assert len(L0) == ZUNITS and ZUNITS % RING == 0


def l0_taken(c, by):
    return sum(u[0] in by for u in L0[:c + 1])


def l0_units():
    units = [("cT", p, c) for p in range(2) for c in range(CH)]
    units += [("pg", 0, 0), ("pg", 0, 1), ("th", 0, 0)]
    for b in range(HB):
        nxt = b + 1 < HB
        units.append(("M", b, 0))
        units += [("pg", b + 1, 0), ("pg", b + 1, 1)] if nxt else []
        units.append(("y", b, 0))
        units += [("th", b + 1, 0)] if nxt else []
        units += [("wy", b, 0), ("wy", b, 1)]
    return units


L0 = l0_units()
assert len(L0) == ZUNITS and ZUNITS % RING == 0


def l0_taken(c, by):
    return sum(u[0] in by for u in L0[:c + 1])


def l0_units():
    units = [("cT", p, c) for p in range(2) for c in range(CH)]
    units += [("pg", 0, 0), ("pg", 0, 1), ("th", 0, 0)]
    for b in range(HB):
        nxt = b + 1 < HB
        units.append(("M", b, 0))
        units += [("pg", b + 1, 0), ("pg", b + 1, 1)] if nxt else []
        units.append(("y", b, 0))
        units += [("th", b + 1, 0)] if nxt else []
        units += [("wy", b, 0), ("wy", b, 1)]
    return units


L0 = l0_units()
assert len(L0) == ZUNITS and ZUNITS % RING == 0


def l0_taken(c, by):
    return sum(u[0] in by for u in L0[:c + 1])


def l0_units():
    units = [("cT", p, c) for p in range(2) for c in range(CH)]
    units += [("pg", 0, 0), ("pg", 0, 1), ("th", 0, 0)]
    for b in range(HB):
        nxt = b + 1 < HB
        units.append(("M", b, 0))
        units += [("pg", b + 1, 0), ("pg", b + 1, 1)] if nxt else []
        units.append(("y", b, 0))
        units += [("th", b + 1, 0)] if nxt else []
        units += [("wy", b, 0), ("wy", b, 1)]
    return units


L0 = l0_units()
assert len(L0) == ZUNITS and ZUNITS % RING == 0


def l0_taken(c, by):
    return sum(u[0] in by for u in L0[:c + 1])


def l0_units():
    units = [("cT", p, c) for p in range(2) for c in range(CH)]
    units += [("pg", 0, 0), ("pg", 0, 1), ("th", 0, 0)]
    for b in range(HB):
        nxt = b + 1 < HB
        units.append(("M", b, 0))
        units += [("pg", b + 1, 0), ("pg", b + 1, 1)] if nxt else []
        units.append(("y", b, 0))
        units += [("th", b + 1, 0)] if nxt else []
        units += [("wy", b, 0), ("wy", b, 1)]
    return units


L0 = l0_units()
assert len(L0) == ZUNITS and ZUNITS % RING == 0


def l0_taken(c, by):
    return sum(u[0] in by for u in L0[:c + 1])


def l0_units():
    units = [("cT", p, c) for p in range(2) for c in range(CH)]
    units += [("pg", 0, 0), ("pg", 0, 1), ("th", 0, 0)]
    for b in range(HB):
        nxt = b + 1 < HB
        units.append(("M", b, 0))
        units += [("pg", b + 1, 0), ("pg", b + 1, 1)] if nxt else []
        units.append(("y", b, 0))
        units += [("th", b + 1, 0)] if nxt else []
        units += [("wy", b, 0), ("wy", b, 1)]
    return units


L0 = l0_units()
assert len(L0) == ZUNITS and ZUNITS % RING == 0


def l0_taken(c, by):
    return sum(u[0] in by for u in L0[:c + 1])


def l0_units():
    units = [("cT", p, c) for p in range(2) for c in range(CH)]
    units += [("pg", 0, 0), ("pg", 0, 1), ("th", 0, 0)]
    for b in range(HB):
        nxt = b + 1 < HB
        units.append(("M", b, 0))
        units += [("pg", b + 1, 0), ("pg", b + 1, 1)] if nxt else []
        units.append(("y", b, 0))
        units += [("th", b + 1, 0)] if nxt else []
        units += [("wy", b, 0), ("wy", b, 1)]
    return units


L0 = l0_units()
assert len(L0) == ZUNITS and ZUNITS % RING == 0


def l0_taken(c, by):
    return sum(u[0] in by for u in L0[:c + 1])


def l0_units():
    units = [("cT", p, c) for p in range(2) for c in range(CH)]
    units += [("pg", 0, 0), ("pg", 0, 1), ("th", 0, 0)]
    for b in range(HB):
        nxt = b + 1 < HB
        units.append(("M", b, 0))
        units += [("pg", b + 1, 0), ("pg", b + 1, 1)] if nxt else []
        units.append(("y", b, 0))
        units += [("th", b + 1, 0)] if nxt else []
        units += [("wy", b, 0), ("wy", b, 1)]
    return units


L0 = l0_units()
assert len(L0) == ZUNITS and ZUNITS % RING == 0


def l0_taken(c, by):
    return sum(u[0] in by for u in L0[:c + 1])


def bass_xattn(nc, x_in, ctx_in, thw, thb, pgw, pgb, www, bncol, wa, wk, wv, wb, hcol, vrow,
               lncol, f1col, orow, out):
    ctx = ExitStack()
    with ctx:
        def sb(name, shape, dt=F32):
            return ctx.enter_context(nc.sbuf_tensor(name, [P, *shape], dt))

        def pair(name, shape):
            return sb(name + "_hi", shape, F32R), sb(name + "_lo", shape, F32R)

        def sem(name):
            return ctx.enter_context(nc.semaphore(name))

        def f(ap):
            return ap.bitcast(F32)

        def over(names_shapes, first, size):
            at, made = first, []
            for name, shape in names_shapes:
                made.append(nc.alloc_sbuf_tensor_at(name, [P, *shape], F32, offset=at))
                at += 4 * int(np.prod(shape))
            assert at <= first + size
            return made

        def next_address():
            return -(-nc.sbuf_base // 32) * 32

        x = sb("x", [TILES, D])
        hT = pair("hT", [CH, HB * TOK])
        cT = pair("cT", [CH, HB * TOK])
        wqs = pair("wqs", [CH, 256])
        wks = pair("wks", [CH, 256])
        wvs = pair("wvs", [CH, 256])
        wos = pair("wos", [2, D])
        raw_q = sb("raw_q", [CH, 256])
        raw_k = sb("raw_k", [CH, 256])
        raw_v = sb("raw_v", [CH, 256])
        raw_o = sb("raw_o", [2, D])
        raw_vb = sb("raw_vb", [2, 256])
        vb = sb("vb", [256])
        PT = pair("PT", [2, 256])
        probs = sb("probs", [2, 2, 258])
        tmp = sb("tmp", [2, 512])
        ident = sb("ident", [P])
        hc = sb("hc", [4, 34])
        bkx = pair("bkx", [34])
        lnc = sb("lnc", [2, 3, CH])
        f1c = sb("f1c", [F // P])
        thb_s = sb("thb_s", [1])
        brow = sb("brow", [D])
        bnc = sb("bnc", [5, 2])
        bns = sb("bns", [2, 2])
        bnt = sb("bnt", [3, 2])
        minus_half = sb("minus_half", [4])
        stats = sb("stats", [4, 6])
        mv = sb("mv", [4, 2])
        vpe = sb("vpe", [4])
        rstd = sb("rstd", [4])
        mx = sb("mx", [2, 2])
        nm = sb("nm", [2, 2])
        sums = sb("sums", [2, 2])
        rs = sb("rs", [2, 2])
        at = next_address()
        qT = pair("qT", [2, 512])
        wth, wpg, www_s, pgb_s = over([("wth", [2, CI]), ("wpg", [2, 2 * CI]), ("www_s", [TOK]),
                                       ("pgb_s", [2 * CI])], at, nc.sbuf_base - at)
        at = next_address()
        kT = pair("kT", [2, 2, 2, 258])
        v = pair("v", [2, 4, 256])
        x0, c0 = over([("x0", [TILES, D]), ("c0", [TILES, D])], at, nc.sbuf_base - at)
        at = next_address()
        oT = pair("oT", [2, 2, 512])
        pg, th, y, msb = over([("pg", [4, 256]), ("th", [D]), ("y", [D]), ("msb", [P])], at, nc.sbuf_base - at)
        z, = over([("z", [4, D])], at, nc.sbuf_base - at)

        U = ctx.enter_context(nc.psum_tensor("U", [P, RING, 512], F32))
        S = ctx.enter_context(nc.psum_tensor("S", [P, 2, 512], F32))
        T = ctx.enter_context(nc.psum_tensor("T", [P, 2, 256], F32))
        O = ctx.enter_context(nc.psum_tensor("O", [P, 512], F32))

        consts_in, l0_in, stored = sem("consts_in"), sem("l0_in"), sem("stored")
        ident_zero, ident_ready = sem("ident_zero"), sem("ident_ready")
        bn_step, bn_rstd, bn_ready = sem("bn_step"), sem("bn_rstd"), sem("bn_ready")
        bk_hi, bk_lo = sem("bk_hi"), sem("bk_lo")
        raw_in = {m: sem("raw_in_" + m) for m in "qkvo"}
        split = {m: sem("split_" + m) for m in "qkvo"}
        hi_part = sem("hi_part")
        z_unit, z_free_v, z_free_a, z_hi, z_x = (sem("z_" + s) for s in ("unit", "free_v", "free_a", "hi", "x"))
        pro_unit, pro_hi, pro_v32, pro_free = (sem("pro_" + s) for s in ("unit", "hi", "v32", "free"))
        ln_stats, ln_mv, ln_eps, ln_rstd, ln_z = (sem("ln_" + s) for s in ("stats", "mv", "eps", "rstd", "z"))
        ln_T, ln_affine, ln_hi, ln_h, ln_bias = (sem("ln_" + s) for s in ("T", "affine", "hi", "h", "bias"))
        brow_in, apart = sem("brow_in"), sem("apart")
        a_unit, a_free, a_hi, a_v32 = (sem("a_" + s) for s in ("unit", "free", "hi", "v32"))
        a_logit, a_T, a_pv = (sem("a_" + s) for s in ("logit", "T", "pv"))
        a_rawmax, a_max, a_exp, a_rcp, a_prob = (sem("a_" + s) for s in ("rawmax", "max", "exp", "rcp", "prob"))
        a_pthi, a_pt, a_ohi, a_o = (sem("a_" + s) for s in ("pthi", "pt", "ohi", "o"))
        m_unit, m_gelu, m_hi, m_act, m_free = (sem("m_" + s) for s in ("unit", "gelu", "hi", "act", "free"))

        block = ctx.enter_context(nc.Block())

        def bank(c):
            return U[:, c % RING, :]

        def qslot(part, h):
            return qT[part][:, h, :]

        def kview(part, p, h):
            return kT[part][:, p, h, :, 0:256]

        def vview(part, p, pair_of):
            return v[part][:, p, 2 * pair_of:2 * pair_of + 2, :]

        def two(ap):
            return ap.rearrange("p (a n) -> p a n", a=2)

        def wait_apart(eng, sem, value):
            eng.wait_ge(sem, value)
            eng.sem_inc(apart, 1)

        @block.sync
        def _(sp):
            for dst, src in ((thb_s, thb), (bnc, bncol), (hc, hcol), (lnc, lncol), (f1c, f1col)):
                sp.dma_start(dst[:], src).then_inc(consts_in, 16)
            sp.dma_start(raw_k[:], wk[0]).then_inc(raw_in["k"], 16)
            sp.dma_start(raw_v[:], wv[0]).then_inc(raw_in["v"], 16)
            sp.dma_start(raw_vb[:], vrow[0].partition_broadcast(P)).then_inc(raw_in["v"], 16)
            sp.dma_start(raw_q[:], wa[0]).then_inc(raw_in["q"], 16)

            def group(w, e):
                return w[bass.ds(e, 1)].rearrange("a p c n -> (a p) c n")

            with sp.Fori(0, HALVES) as half:
                sp.wait_ge(a_unit, half * (UNITS * HBODIES) + CR1)
                for src, dst in ((ctx_in, c0), (x_in, x0)):
                    for p in range(2):
                        sp.dma_start(dst[:, 4 * p:4 * p + 4, :],
                                     src[bass.ds(half * 2 + p, 1)].rearrange("a t p n -> p (a t) n")).then_inc(l0_in, 16)
                for src, dst in ((thw, wth), (pgw, wpg), (www, www_s)):
                    sp.dma_start(dst[:], src).then_inc(l0_in, 16)
                sp.dma_start(pgb_s[:], pgb.partition_broadcast(P)).then_inc(l0_in, 16)
                with sp.Fori(0, LAYERS) as layer:
                    sp.wait_ge(ln_bias, (half * 3 + layer) * TILES + CR1)
                    sp.dma_start(brow[:], orow[bass.ds(layer, 1)].rearrange("a n -> (a n)").partition_broadcast(P)).then_inc(brow_in, 16)
                    with sp.Fori(0, BODIES) as g:
                        e = layer * BODIES + g
                        n = half * HBODIES + e
                        sp.wait_ge(split["o"], half * STREAM + e + CR1)
                        sp.dma_start(raw_o[:], group(wb, e)).then_inc(raw_in["o"], 16)
                        sp.wait_ge(split["k"], n + 1)
                        sp.dma_start(raw_k[:], group(wk, e + 1)).then_inc(raw_in["k"], 16)
                        sp.wait_ge(split["v"], n + 1)
                        sp.dma_start(raw_v[:], group(wv, e + 1)).then_inc(raw_in["v"], 16)
                        sp.dma_start(raw_vb[:], vrow[bass.ds(e + 1, 1)].rearrange("a b n -> (a b) n").partition_broadcast(P)).then_inc(raw_in["v"], 16)
                        sp.wait_ge(split["q"], half * STREAM + e + 1)
                        sp.dma_start(raw_q[:], group(wa, e + 1)).then_inc(raw_in["q"], 16)
                sp.wait_ge(ln_bias, (half * 3 + 2) * TILES + CR1)
                sp.dma_start(brow[:], orow[2].partition_broadcast(P)).then_inc(brow_in, 16)
                with sp.Fori(HBODIES, STREAM) as e:
                    sp.wait_ge(split["o"], half * STREAM + e + CR1)
                    sp.dma_start(raw_o[:], group(wb, e)).then_inc(raw_in["o"], 16)
                    sp.wait_ge(split["q"], half * STREAM + e + 1)
                    sp.dma_start(raw_q[:], group(wa, e + 1)).then_inc(raw_in["q"], 16)

        @block.gpsimd
        def _(pool):
            pool.sem_inc(split["o"], CR1)
            pool.sem_inc(ln_bias, CR1)
            pool.memset(ident[:], 0.0).then_inc(ident_zero, 1)
            pool.memset(minus_half[:], -0.5).then_inc(ident_zero, 1)
            pool.wait_ge(ident_zero, 2)
            pool.affine_select(out=ident[:], in_=ident[:], compare_op=ALU.not_equal, fill=1.0, base=0,
                               pattern=[[-1, P]], channel_multiplier=1).then_inc(ident_ready, 1)
            pool.wait_ge(bn_step, 1)
            pool.tensor_tensor(bnt[:, 1, :], bnt[:, 0, :], minus_half[:, 0:2], ALU.pow).then_inc(bn_rstd, 1)

            def halve(hi_lo, raw, m, count, hi_count):
                wait_apart(pool, raw_in[m], count)
                pool.tensor_copy(hi_lo[0][:], raw[:]).then_inc(hi_part, 1)
                pool.wait_ge(hi_part, hi_count)
                return pool.tensor_tensor(hi_lo[1][:], raw[:], f(hi_lo[0][:]), ALU.subtract)

            def halve_v(done, hi_count):
                halve(wvs, raw_v, "v", 32 * done, hi_count)
                return pool.tensor_tensor(vb[:], raw_vb[:, 0, :], raw_vb[:, 1, :], ALU.subtract)

            halve(wks, raw_k, "k", 16, 1).then_inc(split["k"], 1)
            halve_v(1, 2).then_inc(split["v"], 1)
            halve(wqs, raw_q, "q", 16, 3).then_inc(split["q"], 1)
            HI0 = 3
            HI_HALF = 4 * HBODIES + 2 * MBODIES

            def norm(l):
                for p in range(2):
                    pool.wait_ge(ln_eps, l * 2 + p + 1)
                    pool.tensor_tensor(rstd[:], vpe[:], minus_half[:], ALU.pow).then_inc(ln_rstd, 1)
                pool.wait_ge(brow_in, l * 16 + 16)
                for t in range(TILES):
                    pool.wait_ge(ln_z, l * TILES + t + 1)
                    pool.tensor_tensor(x[:, t, :], x[:, t, :], brow[:], ALU.add).then_inc(ln_bias, 1)

            with pool.Fori(0, HALVES) as half:
                with pool.Fori(0, LAYERS) as layer:
                    norm(half * 3 + layer)
                    with pool.Fori(0, BODIES) as g:
                        e = layer * BODIES + g
                        n = pool.snap(half * HBODIES + e)
                        E = pool.snap(half * STREAM + e)
                        hi0 = pool.snap(half * HI_HALF + e * 4 + HI0)
                        pool.wait_ge(a_unit, n * UNITS + CR1)
                        pool.wait_ge(m_unit, half * (MUNITS * MBODIES) + CR1)
                        halve(wos, raw_o, "o", E * 16 + 16, hi0 + 1).then_inc(split["o"], 1)
                        pool.wait_ge(a_unit, n * UNITS + K11 + 1 + CR1)
                        halve(wks, raw_k, "k", n * 16 + 32, hi0 + 2).then_inc(split["k"], 1)
                        pool.wait_ge(a_free, n * UNITS + V11 + 1 + CR4)
                        halve_v(n + 2, hi0 + 3).then_inc(split["v"], 1)
                        pool.wait_ge(a_unit, n * UNITS + Q11 + 1 + CR1)
                        halve(wqs, raw_q, "q", E * 16 + 32, hi0 + 4).then_inc(split["q"], 1)
                norm(half * 3 + 2)
                with pool.Fori(0, MBODIES) as g:
                    m = pool.snap(half * MBODIES + g)
                    E = pool.snap(half * STREAM + g + HBODIES)
                    hi0 = pool.snap(half * HI_HALF + g * 2 + HI0 + 4 * HBODIES)
                    pool.wait_ge(a_unit, half * (UNITS * HBODIES) + UNITS * HBODIES + CR1)
                    pool.wait_ge(m_unit, m * MUNITS + CR1)
                    halve(wos, raw_o, "o", E * 16 + 16, hi0 + 1).then_inc(split["o"], 1)
                    pool.wait_ge(m_unit, m * MUNITS + 4 + CR1)
                    halve(wqs, raw_q, "q", E * 16 + 32, hi0 + 2).then_inc(split["q"], 1)

        @block.tensor
        def _(pe):
            pe.sem_inc(a_unit, CR1)
            pe.sem_inc(m_unit, CR1)
            pe.sem_inc(a_T, CR2)
            pe.sem_inc(a_pv, CR1)

            def product(o, lhs, rhs, start, stop):
                pe.matmul(o, lhs[0], rhs[0], start=start, stop=False)
                pe.matmul(o, lhs[0], rhs[1], start=False, stop=False)
                return pe.matmul(o, lhs[1], rhs[0], start=False, stop=stop)

            def parts(pr, *ix):
                return tuple(t[(slice(None), *ix)] for t in pr)

            def proj_half(c, w, h, src, p, s):
                for ch in (2 * s, 2 * s + 1):
                    mm = product(bank(c), parts(w, ch, slice(h * P, h * P + P)),
                                 parts(src, ch, slice(p * 512, p * 512 + 512)), ch == 0, ch == CH - 1)
                return mm

            def v_half(c, p, pair_of, s):
                t = p * 512 + (2 * pair_of + s) * P
                for ch in range(CH):
                    mm = product(bank(c)[:, s * 256:s * 256 + 256], parts(cT, ch, slice(t, t + P)),
                                 parts(wvs, ch, slice(0, 256)), ch == 0, ch == CH - 1)
                return mm

            def out_tile(c, p, t):
                for h in range(2):
                    mm = product(bank(c), parts(oT, p, h, slice(t * P, t * P + P)),
                                 parts(wos, h, slice(0, D)), h == 0, h == 1)
                return mm

            def l0(half):
                pe.wait_ge(m_free, half * (8 * MBODIES) + CR4)
                pe.wait_ge(l0_in, half * 128 + 128)
                for c, (kind, b, part) in enumerate(L0):
                    if c >= RING:
                        by = TO_V if L0[c - RING][0] in TO_V else TO_A
                        free, per = (z_free_v, l0_taken(ZUNITS, TO_V)) if by is TO_V else (z_free_a, l0_taken(ZUNITS, TO_A))
                        pe.wait_ge(free, half * per + l0_taken(c - RING, by))
                    nv, na = l0_taken(ZUNITS, TO_V), l0_taken(ZUNITS, TO_A)
                    o = bank(c)
                    if kind == "cT":
                        for t in range(4):
                            mm = pe.transpose(o[:, t * P:t * P + P], c0[:, 4 * b + t, part * P:part * P + P], ident[:])
                    elif kind == "pg":
                        for i in range(2):
                            ch = 2 * part + i
                            for tt in range(2):
                                mm = pe.matmul(o[:, i * 256:i * 256 + 256], c0[:, 2 * b + tt, ch * P:ch * P + P],
                                               wpg[:, tt, :], start=tt == 0, stop=tt == 1)
                    elif kind == "th":
                        for tt in range(2):
                            mm = pe.matmul(o, wth[:, tt, :], x0[:, 2 * b + tt, :], start=tt == 0, stop=tt == 1)
                    elif kind == "M":
                        pe.wait_ge(z_free_v, half * nv + l0_taken(L0.index(("pg", b, 1)), TO_V))
                        for ch in range(CH):
                            mm = pe.matmul(o[:, 0:P], pg[:, ch, 0:P], pg[:, ch, P:2 * P], start=ch == 0, stop=ch == CH - 1)
                    elif kind == "y":
                        pe.wait_ge(z_free_a, half * na + l0_taken(L0.index(("M", b, 0)), TO_A))
                        mm = pe.matmul(o, msb[:], th[:], start=True, stop=True)
                    else:
                        if part == 0:
                            pe.wait_ge(z_free_a, half * na + l0_taken(L0.index(("y", b, 0)), TO_A))
                        mm = pe.matmul(o, www_s[:, part * P:part * P + P], y[:], start=True, stop=True)
                    mm.then_inc(z_unit, 1)

            def prologue(half):
                pe.wait_ge(z_free_v, half * l0_taken(ZUNITS, TO_V) + l0_taken(ZUNITS, TO_V))
                pe.wait_ge(z_free_a, half * l0_taken(ZUNITS, TO_A) + l0_taken(ZUNITS, TO_A))
                pe.wait_ge(split["k"], half * HBODIES + 1)
                pe.wait_ge(split["v"], half * HBODIES + 1)
                for c in range(4):
                    for s in range(2):
                        mm = proj_half(c, wks, c, cT, 0, s) if c < 2 else v_half(c, 0, c - 2, s)
                    mm.then_inc(pro_unit, 1)

            def norm(l, half, bodies):
                pe.wait_ge(pro_free, half * 4 + 4)
                pe.wait_ge(a_free, bodies * UNITS + CR4)
                for k in range(2 * CH):
                    p, ch = k // CH, k % CH
                    if ch == 0:
                        pe.wait_ge(ln_z, l * TILES + 4 * p + 4)
                    if k >= RING:
                        pe.wait_ge(ln_affine, l * 8 + k - RING + 1)
                    for t in range(4):
                        mm = pe.transpose(bank(k)[:, t * P:t * P + P], z[:, t, ch * P:ch * P + P], ident[:])
                    mm.then_inc(ln_T, 1)

            def attention(half, layer, g):
                e = layer * BODIES + g
                n = half * HBODIES + e
                ub = pe.snap(n * UNITS)
                jb = pe.snap(n * ITEMS)
                E = pe.snap(half * STREAM + e)

                def unit(c, s):
                    if s == 0 or c in range(WO0, WO0 + 4) or c >= WO1:
                        pe.wait_ge(a_free, ub + c - RING + 1 + CR4)
                    if c == Q00 and s == 0:
                        pe.wait_ge(split["q"], E + 1)
                        pe.wait_ge(ln_h, half * 24 + layer * 8 + 8 + CR2)
                    if c == KN0 and s == 0:
                        pe.wait_ge(split["k"], n + 2)
                    if c == VN0 and s == 0:
                        pe.wait_ge(split["v"], n + 2)
                    if c in (Q00, Q01, Q10, Q11):
                        mm = proj_half(c, wqs, c % 2, hT, c // Q10, s)
                    elif c in (K10, K11):
                        mm = proj_half(c, wks, c - K10, cT, 1, s)
                    elif c in (KN0, KN1):
                        mm = proj_half(c, wks, c - KN0, cT, 0, s)
                    elif c in (V10, V11):
                        mm = v_half(c, 1, c - V10, s)
                    elif c in (VN0, VN1):
                        mm = v_half(c, 0, c - VN0, s)
                    else:
                        p, t = (0, c - WO0) if c < WO1 else (1, c - WO1)
                        if c == WO0:
                            pe.wait_ge(split["o"], E + 1 + CR1)
                        if t in (0, 2):
                            pe.wait_ge(a_o, jb + 4 * p + (3 if t == 0 else 4) + CR1)
                        mm = out_tile(c, p, t)
                        s = 1
                    if s == 1:
                        mm.then_inc(a_unit, 1)

                def logits(j):
                    p, h, b = item(j)
                    if b == 0:
                        pe.wait_ge(a_free, ub + (Q00, Q01, Q10, Q11)[j // 2] + 1 + CR4)
                    pe.wait_ge(a_exp, jb + j + CR1)
                    for qt in range(2):
                        q0 = b * 256 + qt * P
                        mm = product(S[:, qt, 0:258], parts(qT, h, slice(q0, q0 + P)), parts(kT, p, h, b), True, True)
                    mm.then_inc(a_logit, 1)

                def turn(j):
                    pe.wait_ge(a_prob, jb + j + 1)
                    pe.wait_ge(a_pt, jb + j + CR1)
                    for tt in range(2):
                        for qt in range(2):
                            mm = pe.transpose(T[:, tt, qt * P:qt * P + P],
                                              probs[:, j % 2, qt, tt * P:tt * P + P], ident[:])
                    mm.then_inc(a_T, 1)

                def values(j):
                    p, h, b = item(j)
                    pe.wait_ge(a_pt, jb + j + 1 + CR1)
                    pe.wait_ge(a_o, jb + j + CR1)
                    for tt in range(2):
                        mm = product(O[:, 0:256], parts(v, p, 2 * b + tt, slice(h * P, h * P + P)),
                                     parts(PT, tt), tt == 0, tt == 1)
                    mm.then_inc(a_pv, 1)

                for c in (Q00, Q01):
                    unit(c, 0)
                    unit(c, 1)
                for j in range(ITEMS):
                    logits(j)
                    if j:
                        values(j - 1)
                    unit(*FILL[3 * j])
                    unit(*FILL[3 * j + 1])
                    turn(j)
                    unit(*FILL[3 * j + 2])
                values(ITEMS - 1)
                for t in range(4):
                    unit(WO1 + t, 1)

            def mlp(half, g):
                m = half * MBODIES + g
                ub = pe.snap(m * MUNITS)
                E = pe.snap(half * STREAM + g + HBODIES)
                pe.wait_ge(ln_h, half * 24 + 24 + CR2)
                pe.wait_ge(split["q"], E + 1)
                for c in range(4):
                    pe.wait_ge(m_free, m * 8 + c - 3 + CR4)
                    for s in range(2):
                        mm = proj_half(c, wqs, c % 2, hT, c // 2, s)
                    mm.then_inc(m_unit, 1)
                pe.wait_ge(split["o"], E + 1 + CR1)
                for c in range(4, MUNITS):
                    p, t = (c - 4) // 4, c % 4
                    if t == 0:
                        pe.wait_ge(m_act, m * 4 + 2 * p + 2 + CR2)
                    if c < 8:
                        pe.wait_ge(m_gelu, m * 4 + c - 3)
                    else:
                        pe.wait_ge(m_free, m * 8 + c - 7 + CR4)
                    out_tile(c, p, t).then_inc(m_unit, 1)

            pe.wait_ge(ident_ready, 1)
            with pe.Fori(0, HALVES) as half:
                l0(half)
                prologue(half)
                with pe.Fori(0, LAYERS) as layer:
                    norm(half * 3 + layer, half, half * HBODIES + layer * BODIES)
                    with pe.Fori(0, BODIES) as g:
                        attention(half, layer, g)
                norm(half * 3 + 2, half, half * HBODIES + HBODIES)
                with pe.Fori(0, MBODIES) as g:
                    mlp(half, g)

        @block.scalar
        def _(act):
            act.sem_inc(a_exp, CR1)
            act.sem_inc(stored, CR1)
            act.wait_ge(consts_in, 16 * 5)
            act.activation(bkx[0][:], hc[:, 2, :], ACT.Copy).then_inc(bk_hi, 1)
            ZU_A, ZU_V = l0_taken(ZUNITS, TO_A), l0_taken(ZUNITS, TO_V)

            def l0(half):
                for c, (kind, b, part) in enumerate(L0):
                    o = bank(c)
                    if kind == "pg":
                        continue
                    act.wait_ge(z_unit, half * ZUNITS + c + 1)
                    if kind == "cT":
                        act.activation(cT[0][:, part, b * 512:b * 512 + 512], o, ACT.Copy).then_inc(z_hi, 1)
                    elif kind == "th":
                        act.activation(th[:], o, ACT.Identity, bias=thb_s[:, 0:1]).then_inc(z_free_a, 1)
                    elif kind == "M":
                        act.activation(msb[:], o[:, 0:P], ACT.Copy, scale=1.0 / D).then_inc(z_free_a, 1)
                    elif kind == "y":
                        act.activation(y[:], o, ACT.Copy).then_inc(z_free_a, 1)
                    else:
                        k = 2 * b + part
                        if k == 0:
                            act.wait_ge(bn_ready, 1)
                        act.wait_ge(z_x, half * TILES + k - 1 + CR2)
                        act.activation(tmp[:, part, :], o, ACT.Identity, bias=bns[:, 1, part:part + 1],
                                       scale=bns[:, 0, part:part + 1]).then_inc(z_free_a, 1)

            def kv_hi(c, p, h, waits, b, count, hi, v32, col):
                if h < 2:
                    act.wait_ge(waits, count)
                    act.activation(kview(0, p, h), two(bank(c)), ACT.Identity, bias=col).then_inc(hi, 1)
                else:
                    act.wait_ge(v32, b)
                    act.activation(vview(0, p, h - 2), two(tmp[:, h - 2, :]), ACT.Copy).then_inc(hi, 1)

            def norm(l):
                for k in range(2 * CH):
                    p, ch = k // CH, k % CH
                    li = layer_of[0]
                    wait_apart(act, ln_T, l * 8 + k + 1)
                    wait_apart(act, ln_h, l * 8 + k - 1 + CR2)
                    act.activation(tmp[:, k % 2, :], bank(k), ACT.Identity, bias=lnc[:, 1, li, ch:ch + 1] if isinstance(li, int) else lnc[:, 1, bass.ds(li, 1), ch],
                                   scale=lnc[:, 0, li, ch:ch + 1] if isinstance(li, int) else lnc[:, 0, bass.ds(li, 1), ch]).then_inc(ln_affine, 1)

            layer_of = [None]

            def attention(half, layer, g):
                e = layer * BODIES + g
                n = half * HBODIES + e
                ub = act.snap(n * UNITS)
                jb = act.snap(n * ITEMS)
                hb = act.snap(n * 12)
                vb4 = act.snap(n * 4)
                head = act.snap(e * 2)
                order = [Q00, Q01, K10, K11, V10, V11, Q10, Q11, KN0, KN1, VN0, VN1]

                def unit_hi(c):
                    if c not in order:
                        return
                    if c in (Q00, Q01, Q10, Q11):
                        wait_apart(act, a_unit, ub + c + 1 + CR1)
                        act.activation(qslot(0, c % 2), bank(c), ACT.Identity,
                                       bias=hc[:, 0, bass.ds(head + c % 2, 1)]).then_inc(a_hi, 1)
                    elif c in (K10, K11, KN0, KN1):
                        h, p, ahead = c % 2, int(c < KN0), 2 * int(c >= KN0)
                        wait_apart(act, a_unit, ub + c + 1 + CR1)
                        act.activation(kview(0, p, h), two(bank(c)), ACT.Identity,
                                       bias=hc[:, 1, bass.ds(head + h + ahead, 1)]).then_inc(a_hi, 1)
                    else:
                        i = (V10, V11, VN0, VN1).index(c)
                        act.wait_ge(a_v32, vb4 + i + 1)
                        act.activation(vview(0, int(c < VN0), i % 2), two(tmp[:, i % 2, :]), ACT.Copy).then_inc(a_hi, 1)

                def o_hi(j):
                    p, h, b = item(j)
                    wait_apart(act, a_pv, jb + j + 1 + CR1)
                    act.activation(oT[0][:, p, h, b * 256:b * 256 + 256], O[:, 0:256], ACT.Identity,
                                   bias=hc[:, 3, bass.ds(head + h, 1)]).then_inc(a_ohi, 1)

                unit_hi(Q00)
                unit_hi(Q01)
                for j in range(ITEMS):
                    act.wait_ge(a_max, jb + j + 1)
                    act.wait_ge(a_T, jb + j - 1 + CR2)
                    for qt in range(2):
                        ins = act.activation(probs[:, j % 2, qt, 0:257], S[:, qt, 0:257], ACT.Exp,
                                             bias=nm[:, j % 2, qt:qt + 1], scale=SCALE,
                                             accum_out=sums[:, j % 2, qt:qt + 1])
                    ins.then_inc(a_exp, 1)
                    if j:
                        o_hi(j - 1)
                    for c in ended(j, False):
                        unit_hi(c)
                    act.wait_ge(a_T, jb + j + 1 + CR2)
                    act.wait_ge(a_pv, jb + j + CR1)
                    act.activation(PT[0][:], T[:], ACT.Copy).then_inc(a_pthi, 1)
                    for c in ended(j, True):
                        unit_hi(c)
                o_hi(ITEMS - 1)

            def mlp(half, g):
                m = half * MBODIES + g
                for c in range(4):
                    wait_apart(act, m_unit, m * MUNITS + c + 1 + CR1)
                    wait_apart(act, m_act, m * 4 + c - 1 + CR2)
                    act.activation(tmp[:, c % 2, :], bank(c), ACT.Gelu,
                                   bias=f1c[:, bass.ds(g * 2 + c % 2, 1)]).then_inc(m_gelu, 1)

            with act.Fori(0, HALVES) as half:
                l0(half)
                act.wait_ge(z_x, half * TILES + TILES + CR2)
                for c in range(4):
                    kv_hi(c, 0, c, pro_unit, half * 2 + c - 1, half * 4 + c + 1, pro_hi, pro_v32, hc[:, 1, c % 2:c % 2 + 1])
                with act.Fori(0, LAYERS) as layer:
                    layer_of[0] = layer
                    norm(half * 3 + layer)
                    with act.Fori(0, BODIES) as g:
                        attention(half, layer, g)
                layer_of[0] = 2
                norm(half * 3 + 2)
                with act.Fori(0, MBODIES) as g:
                    mlp(half, g)
                act.wait_ge(m_free, half * (8 * MBODIES) + 8 * MBODIES + CR4)
                for p in range(2):
                    act.dma_start(out[bass.ds(half * 2 + p, 1)].rearrange("a t p n -> p (a t) n"),
                                  x[:, 4 * p:4 * p + 4, :]).then_inc(stored, 16)
            act.wait_ge(stored, HALVES * 32 + CR1)

        @block.vector
        def _(dve):
            for s, k in ((m_free, CR4), (a_free, CR4), (z_x, CR2), (ln_h, CR2), (a_pt, CR1), (a_o, CR1), (m_act, CR2)):
                dve.sem_inc(s, k)
            dve.wait_ge(consts_in, 16 * 5)
            dve.tensor_scalar(bnt[:, 0, :], bnc[:, 3, :], EPS, None, ALU.add).then_inc(bn_step, 1)
            dve.wait_ge(bn_rstd, 1)
            dve.tensor_tensor(bns[:, 0, :], bnc[:, 0, :], bnt[:, 1, :], ALU.mult).then_inc(bn_step, 1)
            dve.tensor_tensor(bnt[:, 2, :], bnc[:, 4, :], bnc[:, 2, :], ALU.subtract).then_inc(bn_step, 1)
            dve.wait_ge(bn_step, 3)
            dve.tensor_tensor(bnt[:, 2, :], bnt[:, 2, :], bns[:, 0, :], ALU.mult).then_inc(bn_step, 1)
            dve.wait_ge(bn_step, 4)
            dve.tensor_tensor(bns[:, 1, :], bnt[:, 2, :], bnc[:, 1, :], ALU.add).then_inc(bn_ready, 1)
            dve.wait_ge(bk_hi, 1)
            dve.tensor_tensor(bkx[1][:], hc[:, 2, :], f(bkx[0][:]), ALU.subtract).then_inc(bk_lo, 1)
            dve.wait_ge(bk_lo, 1)

            def l0(half):
                his = xs = 0
                for c, (kind, b, part) in enumerate(L0):
                    o = bank(c)
                    if kind == "cT":
                        his += 1
                        dve.wait_ge(z_hi, half * 8 + his)
                        to = slice(b * 512, b * 512 + 512)
                        dve.tensor_tensor(cT[1][:, part, to], o, f(cT[0][:, part, to]), ALU.subtract).then_inc(z_free_v, 1)
                    elif kind == "pg":
                        dve.wait_ge(z_unit, half * ZUNITS + c + 1)
                        dve.tensor_tensor(pg[:, 2 * part:2 * part + 2, :], two(o),
                                          pgb_s[:].unsqueeze(1).to_broadcast([P, 2, 256]), ALU.add).then_inc(z_free_v, 1)
                    elif kind == "wy":
                        k = 2 * b + part
                        if k == 0:
                            dve.wait_ge(stored, half * 32 + CR1)
                        dve.wait_ge(z_free_a, half * l0_taken(ZUNITS, TO_A) + l0_taken(c, TO_A))
                        dve.tensor_tensor(x[:, k, :], tmp[:, part, :], x0[:, k, :], ALU.add).then_inc(z_x, 1)

            def k_lo(c, p, h, hi, hi_count, col, bk_col):
                for part in range(2):
                    dve.tensor_copy(kT[part][:, p, h, :, 256:258],
                                    bk_col(f(bkx[part][:])).unsqueeze(2).to_broadcast([P, 2, 2]))
                dve.wait_ge(hi, hi_count)
                return dve.scalar_tensor_tensor(out=kview(1, p, h), in0=two(bank(c)), scalar=col,
                                                in1=f(kview(0, p, h)), op0=ALU.add, op1=ALU.subtract)

            def v_lo(c, p, i, v32, v_count, hi, hi_count):
                dve.tensor_tensor(two(tmp[:, i, :]), two(bank(c)), vb[:].unsqueeze(1).to_broadcast([P, 2, 256]),
                                  ALU.add).then_inc(v32, 1)
                dve.wait_ge(v32, v_count)
                dve.wait_ge(hi, hi_count)
                return dve.tensor_tensor(vview(1, p, i), two(tmp[:, i, :]), f(vview(0, p, i)), ALU.subtract)

            def prologue(half):
                dve.wait_ge(z_x, half * TILES + TILES + CR2)
                for c in range(4):
                    dve.wait_ge(pro_unit, half * 4 + c + 1)
                    if c < 2:
                        ins = k_lo(c, 0, c, pro_hi, half * 4 + c + 1, hc[:, 1, c:c + 1], lambda t, c=c: t[:, c:c + 1])
                    else:
                        ins = v_lo(c, 0, c - 2, pro_v32, half * 2 + c - 1, pro_hi, half * 4 + c + 1)
                    ins.then_inc(pro_free, 1)

            def norm(l, half, bodies):
                dve.wait_ge(z_x, half * TILES + TILES + CR2)
                dve.wait_ge(a_free, bodies * UNITS + CR4)

                def moments(p):
                    for t in range(4):
                        dve.bn_stats(stats[:, t, :], x[:, 4 * p + t, :]).then_inc(ln_stats, 1)
                    for t in range(4):
                        wait_apart(dve, ln_stats, l * 8 + 4 * p + t + 1)
                        dve.bn_aggr(mv[:, t, :], stats[:, t, :]).then_inc(ln_mv, 1)
                    dve.wait_ge(ln_mv, l * 8 + 4 * p + 4)
                    dve.tensor_scalar(vpe[:], mv[:, :, 1], EPS, None, ALU.add).then_inc(ln_eps, 1)

                def normalise(p):
                    dve.wait_ge(ln_rstd, l * 2 + p + 1)
                    if p:
                        dve.wait_ge(ln_T, l * 8 + 4)
                    for t in range(4):
                        dve.tensor_scalar(z[:, t, :], x[:, 4 * p + t, :], mv[:, t, 0:1], rstd[:, t:t + 1],
                                          ALU.subtract, ALU.mult).then_inc(ln_z, 1)

                def spread(p):
                    for ch in range(CH):
                        k = p * CH + ch
                        to = slice(p * 512, p * 512 + 512)
                        dve.wait_ge(ln_affine, l * 8 + k + 1)
                        dve.tensor_copy(hT[0][:, ch, to], tmp[:, k % 2, :]).then_inc(ln_hi, 1)
                        dve.wait_ge(ln_hi, l * 8 + k + 1)
                        dve.tensor_tensor(hT[1][:, ch, to], tmp[:, k % 2, :], f(hT[0][:, ch, to]), ALU.subtract).then_inc(ln_h, 1)

                moments(0)
                normalise(0)
                dve.wait_ge(ln_z, l * 8 + 4)
                moments(1)
                spread(0)
                normalise(1)
                spread(1)

            def attention(half, layer, g):
                e = layer * BODIES + g
                n = half * HBODIES + e
                ub = dve.snap(n * UNITS)
                jb = dve.snap(n * ITEMS)
                hb = dve.snap(n * 12)
                vb4 = dve.snap(n * 4)
                head = dve.snap(e * 2)
                order = [Q00, Q01, K10, K11, V10, V11, Q10, Q11, KN0, KN1, VN0, VN1]
                vs = (V10, V11, VN0, VN1)

                def unit_lo(c):
                    hi_count = hb + order.index(c) + 1 if c in order else None
                    if c in (Q00, Q01, Q10, Q11):
                        dve.wait_ge(a_hi, hi_count)
                        ins = dve.scalar_tensor_tensor(out=qslot(1, c % 2), in0=bank(c), scalar=hc[:, 0, bass.ds(head + c % 2, 1)],
                                                       in1=f(qslot(0, c % 2)), op0=ALU.add, op1=ALU.subtract)
                    elif c in (K10, K11, KN0, KN1):
                        h, p, ahead = c % 2, int(c < KN0), 2 * int(c >= KN0)
                        dve.wait_ge(a_unit, ub + c + 1 + CR1)
                        ins = k_lo(c, p, h, a_hi, hi_count, hc[:, 1, bass.ds(head + h + ahead, 1)],
                                   lambda t: t[:, bass.ds(head + h + ahead, 1)])
                    elif c in vs:
                        i = vs.index(c)
                        if i == 0:
                            dve.wait_ge(split["v"], n + 1)
                        if i == 2:
                            dve.wait_ge(split["v"], n + 2)
                        dve.wait_ge(a_unit, ub + c + 1 + CR1)
                        ins = v_lo(c, int(c < VN0), i % 2, a_v32, vb4 + i + 1, a_hi, hi_count)
                    else:
                        if c == WO0:
                            dve.wait_ge(ln_bias, half * 24 + layer * 8 + 8 + CR1)
                        t = c - WO0 if c < WO1 else 4 + c - WO1
                        dve.wait_ge(a_unit, ub + c + 1 + CR1)
                        ins = dve.tensor_tensor(x[:, t, :], x[:, t, :], bank(c), ALU.add)
                    ins.then_inc(a_free, 1)

                def o_lo(j):
                    p, h, b = item(j)
                    to = slice(b * 256, b * 256 + 256)
                    dve.wait_ge(a_ohi, jb + j + 1)
                    dve.scalar_tensor_tensor(out=oT[1][:, p, h, to], in0=O[:, 0:256], scalar=hc[:, 3, bass.ds(head + h, 1)],
                                             in1=f(oT[0][:, p, h, to]), op0=ALU.add, op1=ALU.subtract).then_inc(a_o, 1)

                unit_lo(Q00)
                unit_lo(Q01)
                for j in range(ITEMS):
                    r = j % 2
                    dve.wait_ge(a_logit, jb + j + 1)
                    dve.tensor_reduce(mx[:, r, :], S[:, :, 0:257], AX.X, ALU.max).then_inc(a_rawmax, 1)
                    dve.wait_ge(a_rawmax, jb + j + 1)
                    dve.tensor_scalar(nm[:, r, :], mx[:, r, :], -SCALE, None, ALU.mult).then_inc(a_max, 1)
                    dve.wait_ge(a_exp, jb + j + 1 + CR1)
                    dve.reciprocal(rs[:, r, :], sums[:, r, :]).then_inc(a_rcp, 1)
                    dve.wait_ge(a_rcp, jb + j + 1)
                    for qt in range(2):
                        ins = dve.tensor_scalar(probs[:, r, qt, 0:256], probs[:, r, qt, 0:256], rs[:, r, qt:qt + 1], None, ALU.mult)
                    ins.then_inc(a_prob, 1)
                    if j:
                        o_lo(j - 1)
                    for c in ended(j, False):
                        unit_lo(c)
                    dve.wait_ge(a_pthi, jb + j + 1)
                    dve.tensor_tensor(PT[1][:], T[:], f(PT[0][:]), ALU.subtract).then_inc(a_pt, 1)
                    for c in ended(j, True):
                        unit_lo(c)
                o_lo(ITEMS - 1)
                for t in range(4):
                    unit_lo(WO1 + t)

            def mlp(half, g):
                m = half * MBODIES + g
                for c in range(4):
                    p, fi = c // 2, c % 2
                    dve.wait_ge(m_gelu, m * 4 + c + 1)
                    dve.tensor_copy(oT[0][:, p, fi, :], tmp[:, c % 2, :]).then_inc(m_hi, 1)
                    dve.wait_ge(m_hi, m * 4 + c + 1)
                    dve.tensor_tensor(oT[1][:, p, fi, :], tmp[:, c % 2, :], f(oT[0][:, p, fi, :]), ALU.subtract).then_inc(m_act, 1)
                dve.wait_ge(ln_bias, half * 24 + 24 + CR1)
                for c in range(4, MUNITS):
                    dve.wait_ge(m_unit, m * MUNITS + c + 1 + CR1)
                    dve.tensor_tensor(x[:, c - 4, :], x[:, c - 4, :], bank(c), ALU.add).then_inc(m_free, 1)

            with dve.Fori(0, HALVES) as half:
                l0(half)
                prologue(half)
                with dve.Fori(0, LAYERS) as layer:
                    norm(half * 3 + layer, half, half * HBODIES + layer * BODIES)
                    with dve.Fori(0, BODIES) as g:
                        attention(half, layer, g)
                norm(half * 3 + 2, half, half * HBODIES + HBODIES)
                with dve.Fori(0, MBODIES) as g:
                    mlp(half, g)


def _laid_out(i):
    a = {k.replace("L0_xattn_", "").replace("L1_xattn_", "L1"): np.ascontiguousarray(v) for k, v in i.items()}

    def col(vec):
        return vec.reshape(-1, P).T

    def heads(*vecs):
        c = col(np.concatenate([v.reshape(-1) for v in vecs]))
        return np.concatenate([c, c[:, :2]], 1)

    def in_groups(w):
        return w.reshape(CH, P, -1, 256).transpose(2, 1, 0, 3)

    def out_groups(w):
        return w.reshape(-1, 2, P, D).transpose(0, 2, 1, 3)

    def both(name):
        return [a[f"L1{name}1"], a[f"L1{name}2"]]

    q = np.concatenate([in_groups(w) for w in both("wq")] + [in_groups(a["L1w_fc1"])])
    k, v = (np.concatenate([in_groups(w) for w in both(s)]) for s in ("wk", "wv"))
    vr = np.stack([np.concatenate([r.reshape(-1) for r in both(s)]).reshape(HBODIES, 256) for s in ("bv", "bias_v")], 1)
    tiles = (HALVES * 2, 4, P, D)
    lns = [[a[f"L1ln{n}_{s}"] for n in ("1", "2", "_mlp")] for s in ("scale", "offset")]
    return {
        "x_in": a["x"].reshape(tiles),
        "ctx_in": a["ctx_2048"].reshape(tiles),
        "thw": a["theta_w"].T.reshape(2, P, CI).transpose(1, 0, 2),
        "thb": col(a["theta_b"]),
        "pgw": np.concatenate([a["phi_w"].T, a["g_w"].T], 1).reshape(2, P, 2 * CI).transpose(1, 0, 2),
        "pgb": np.concatenate([a["phi_b"], a["g_b"]]),
        "www": a["w_w"].T,
        "bncol": np.stack([col(a[s]) for s in ("bn_gamma", "bn_beta", "bn_mean", "bn_var", "w_b")], 1),
        "wa": np.concatenate([q, q[:1]]),
        "wk": np.concatenate([k, k[:1]]),
        "wv": np.concatenate([v, v[:1]]),
        "wb": np.concatenate([out_groups(w) for w in both("wo")] + [out_groups(a["L1w_fc2"])]),
        "hcol": np.stack([heads(*both(s)) for s in ("bq", "bk", "bias_k", "bias_v")], 1),
        "vrow": np.concatenate([vr, vr[:1]]),
        "lncol": np.stack([np.stack([col(x) for x in r], 1) for r in lns], 1),
        "f1col": col(a["L1b_fc1"]),
        "orow": np.stack([*both("bo"), a["L1b_fc2"]]),
    }


def kernel(**inputs):
    import concourse.bacc as bacc
    from concourse.bass_utils import run_bass_kernel_spmd

    nc = bacc.Bacc("TRN2", target_bir_lowering=False, num_devices=1)
    arrays = {k: np.ascontiguousarray(v) for k, v in _laid_out(inputs).items()}
    args = [nc.dram_tensor(k, v.shape, mybir.dt.from_np(v.dtype), kind="ExternalInput").ap() for k, v in arrays.items()]
    out = nc.dram_tensor("out", (HALVES * 2, 4, P, D), F32, kind="ExternalOutput").ap()
    bass_xattn(nc, *args, out)
    r = run_bass_kernel_spmd(nc, [arrays], core_ids=[0])
    return r.results[0]["out"].reshape(B, TOK, D)
```

```python
from contextlib import ExitStack

import numpy as np
import concourse.bass as bass
from concourse import mybir

F32 = mybir.dt.float32
F32R = mybir.dt.float32r
ALU = mybir.AluOpType
ACT = mybir.ActivationFunctionType
AX = mybir.AxisListType

B, TOK, D = 8, 256, 512
CI = 128
H, K, F = 16, 128, 2048
P = 128
EPS = 1e-5
HALVES = 2
HB = B // HALVES
TILES = HB * TOK // P
CH = D // P
LAYERS = 2
BODIES = H // 2
MBODIES = F // 256
HBODIES = LAYERS * BODIES
STREAM = HBODIES + MBODIES
SCALE = float(1.0 / np.sqrt(np.float32(K)))

ITEMS = 8
RING = 4
CR4, CR2, CR1 = 4, 2, 1

UNITS_A = [("q", 0, 0), ("q", 0, 1), ("k", 1, 0), ("k", 1, 1), ("v", 1, 0), ("v", 1, 1), ("q", 1, 0), ("q", 1, 1),
           ("w", 0, 0), ("w", 0, 1), ("K", 0, 0), ("w", 0, 2), ("w", 0, 3), ("K", 0, 1), ("V", 0, 0), ("V", 0, 1),
           ("w", 1, 0), ("w", 1, 1), ("w", 1, 2), ("w", 1, 3)]
UNITS = len(UNITS_A)
UNIT = {u: c for c, u in enumerate(UNITS_A)}
HI_UNITS = [c for c, u in enumerate(UNITS_A) if u[0] != "w"]
V_UNITS = [c for c, u in enumerate(UNITS_A) if u[0] in "vV"]
UNITS_M = {first: [("f", 0, 0), ("f", 0, 1)] + rest for first, rest in (
    (True, [("w", 0, t) for t in range(4)] + [("f", 1, 0), ("f", 1, 1)] + [("w", 1, t) for t in range(4)]),
    (False, [("f", 1, 0), ("f", 1, 1)] + [("w", p, t) for p in range(2) for t in range(4)]))}
MUNITS = 12
FIRST, MIDDLE, LAST = range(3)
W0_END = UNIT["w", 0, 3]


def steps(kind):
    halves = [(c, s) for c in range(2, 16) for s in ((1,) if UNITS_A[c][0] == "w" else (0, 1))]
    out = [("U", c, s) for c in (0, 1) for s in (0, 1)]

    def fill(n):
        for _ in range(n):
            out.append(("U", *halves.pop(0)))

    for j in range(ITEMS):
        out.append(("L", j))
        if j == 0:
            fill(3)
            continue
        out.append(("T", j - 1))
        fill(1)
        if (kind, j) in ((FIRST, 1), (LAST, ITEMS - 1)):
            out.append(("Z", kind == FIRST))
        fill(1)
        out.append(("P", j - 1))
        fill(1)
    out.append(("T", ITEMS - 1))
    assert not halves
    w = [("U", UNIT["w", 1, t], 1) for t in range(4)]
    return out + [w[0], ("P", ITEMS - 1), *w[1:]]


def item(j):
    return j // 4, (j % 4) // 2, j % 2


ZUNITS = 2 * CH + 7 * HB
TO_V, TO_A = ("cT", "pg"), ("th", "M", "y", "wy")


def l0_units():
    units = [("pg", 0, 0), ("pg", 0, 1), ("th", 0, 0)]
    turns = [("cT", p, c) for p in range(2) for c in range(CH)]
    for b in range(HB):
        nxt = b + 1 < HB
        units += [("M", b, 0), turns.pop(0)]
        units += [("pg", b + 1, 0), ("pg", b + 1, 1)] if nxt else []
        units += [("y", b, 0), turns.pop(0)]
        units += [("th", b + 1, 0)] if nxt else []
        units += [("wy", b, 0), ("wy", b, 1)]
    return units


L0 = l0_units()
assert len(L0) == ZUNITS and ZUNITS % RING == 0


def l0_taken(c, by):
    return sum(u[0] in by for u in L0[:c + 1])


def bass_xattn(nc, x_in, ctx_in, thw, thb, pgw, pgb, www, bncol, wa, wk, wv, wb, hcol, vrow,
               lncol, f1col, orow, out):
    ctx = ExitStack()
    with ctx:
        def sb(name, shape, dt=F32):
            return ctx.enter_context(nc.sbuf_tensor(name, [P, *shape], dt))

        def pair(name, shape):
            return sb(name + "_hi", shape, F32R), sb(name + "_lo", shape, F32R)

        def sem(name):
            return ctx.enter_context(nc.semaphore(name))

        def f(ap):
            return ap.bitcast(F32)

        def over(names_shapes, first, size):
            at, made = first, []
            for name, shape in names_shapes:
                made.append(nc.alloc_sbuf_tensor_at(name, [P, *shape], F32, offset=at))
                at += 4 * int(np.prod(shape))
            assert at <= first + size
            return made

        def next_address():
            return -(-nc.sbuf_base // 32) * 32

        x = sb("x", [TILES, D])
        hT = pair("hT", [CH, HB * TOK])
        cT = pair("cT", [CH, HB * TOK])
        wqs = pair("wqs", [CH, 256])
        wks = pair("wks", [CH, 256])
        wvs = pair("wvs", [CH, 256])
        wos = pair("wos", [2, D])
        raw_ok = sb("raw_ok", [CH, 256])
        raw_vq = sb("raw_vq", [CH, 256])
        z = sb("z", [4, D])
        aff = sb("aff", [2, 512])
        raw_vb = sb("raw_vb", [2, 256])
        vb = sb("vb", [256])
        PT = pair("PT", [2, 256])
        probs = sb("probs", [2, 2, 258])
        tmp = sb("tmp", [2, 512])
        ident = sb("ident", [P])
        hc = sb("hc", [4, 34])
        bkx = pair("bkx", [34])
        lnc = sb("lnc", [2, 3 * CH])
        f1c = sb("f1c", [F // P])
        thb_s = sb("thb_s", [1])
        brow = sb("brow", [D])
        bnc = sb("bnc", [5, 2])
        bns = sb("bns", [2, 2])
        bnt = sb("bnt", [3, 2])
        minus_half = sb("minus_half", [4])
        stats = sb("stats", [4, 6])
        mv = sb("mv", [4, 2])
        vpe = sb("vpe", [4])
        rstd = sb("rstd", [4])
        mx = sb("mx", [2, 2])
        nm = sb("nm", [2, 2])
        sums = sb("sums", [2, 2])
        rs = sb("rs", [2, 2])
        at = next_address()
        qT = pair("qT", [2, 512])
        wth, wpg, www_s, pgb_s = over([("wth", [2, CI]), ("wpg", [2, 2 * CI]), ("www_s", [TOK]),
                                       ("pgb_s", [2 * CI])], at, nc.sbuf_base - at)
        at = next_address()
        kT = pair("kT", [2, 2, 2, 258])
        v = pair("v", [2, 4, 256])
        x0, c0 = over([("x0", [TILES, D]), ("c0", [TILES, D])], at, nc.sbuf_base - at)
        at = next_address()
        oT = pair("oT", [2, 2, 512])
        pg, th, y, msb = over([("pg", [4, 256]), ("th", [D]), ("y", [D]), ("msb", [P])], at, nc.sbuf_base - at)

        U = ctx.enter_context(nc.psum_tensor("U", [P, RING, 512], F32))
        S = ctx.enter_context(nc.psum_tensor("S", [P, 2, 512], F32))
        T = ctx.enter_context(nc.psum_tensor("T", [P, 2, 256], F32))
        O = ctx.enter_context(nc.psum_tensor("O", [P, 512], F32))

        consts_in, stored = sem("consts_in"), sem("stored")
        l0_c, l0_x = ([sem(f"l0_{m}{b}") for b in range(HB)] for m in "cx")
        l0_w = sem("l0_w")
        ident_zero, ident_ready = sem("ident_zero"), sem("ident_ready")
        bn_step, bn_rstd, bn_ready = sem("bn_step"), sem("bn_rstd"), sem("bn_ready")
        bk_hi, bk_lo = sem("bk_hi"), sem("bk_lo")
        raw_in = {m: sem("raw_in_" + m) for m in "qkvo"}
        split = {m: sem("split_" + m) for m in "qkvo"}
        hi_part = sem("hi_part")
        z_unit, z_free_v, z_free_a, z_hi, z_x = (sem("z_" + s) for s in ("unit", "free_v", "free_a", "hi", "x"))
        pro_unit, pro_hi, pro_v32, pro_free = (sem("pro_" + s) for s in ("unit", "hi", "v32", "free"))
        ln_stats, ln_mv, ln_eps, ln_rstd, ln_z = (sem("ln_" + s) for s in ("stats", "mv", "eps", "rstd", "z"))
        ln_T, ln_affine, ln_hi, ln_h, ln_bias = (sem("ln_" + s) for s in ("T", "affine", "hi", "h", "bias"))
        brow_in, apart = sem("brow_in"), sem("apart")
        a_unit, a_free, a_hi, a_v32 = (sem("a_" + s) for s in ("unit", "free", "hi", "v32"))
        a_logit, a_T, a_pv = (sem("a_" + s) for s in ("logit", "T", "pv"))
        a_rawmax, a_max, a_exp, a_rcp, a_prob = (sem("a_" + s) for s in ("rawmax", "max", "exp", "rcp", "prob"))
        a_pthi, a_pt, a_ohi, a_o = (sem("a_" + s) for s in ("pthi", "pt", "ohi", "o"))
        m_unit, m_gelu, m_hi, m_act, m_free = (sem("m_" + s) for s in ("unit", "gelu", "hi", "act", "free"))

        block = ctx.enter_context(nc.Block())

        def bank(c):
            return U[:, c % RING, :]

        def qslot(part, h):
            return qT[part][:, h, :]

        def kview(part, p, h):
            return kT[part][:, p, h, :, 0:256]

        def vview(part, p, pair_of):
            return v[part][:, p, 2 * pair_of:2 * pair_of + 2, :]

        def two(ap):
            return ap.rearrange("p (a n) -> p a n", a=2)

        def wait_apart(eng, sem, value):
            eng.wait_ge(sem, value)
            eng.sem_inc(apart, 1)

        @block.sync
        def _(sp):
            def group(w, e):
                return w[bass.ds(e, 1)].rearrange("a p c n -> (a p) c n")

            def l0_inputs(half):
                for src, dst in ((pgw, wpg), (thw, wth), (www, www_s)):
                    sp.dma_start(dst[:], src).then_inc(l0_w, 16)
                sp.dma_start(pgb_s[:], pgb.partition_broadcast(P)).then_inc(l0_w, 16)
                for b in range(HB):
                    for src, dst, s in ((ctx_in, c0, l0_c), (x_in, x0, l0_x)):
                        sp.dma_start(dst[:, 2 * b:2 * b + 2, :],
                                     src[half * 2 + b // 2, 2 * (b % 2):2 * (b % 2) + 2].rearrange("t p n -> p t n")).then_inc(s[b], 16)
                    if (half, b) == (0, 0):
                        for dst, src in ((thb_s, thb), (bnc, bncol), (hc, hcol), (lnc, lncol), (f1c, f1col)):
                            sp.dma_start(dst[:], src).then_inc(consts_in, 16)

            def bias_row(l, row):
                sp.wait_ge(ln_bias, l * TILES + CR1)
                sp.dma_start(brow[:], orow[bass.ds(row, 1)].rearrange("a n -> (a n)").partition_broadcast(P)).then_inc(brow_in, 16)

            def weights(half, layer, g):
                e = layer * BODIES + g
                n = sp.snap(half * HBODIES + e)
                E = sp.snap(half * STREAM + e)
                wait_apart(sp, split["k"], n + 1)
                sp.wait_ge(split["o"], E + CR1)
                sp.dma_start(raw_ok[:], group(wb, e).rearrange("p c (a n) -> p (c a) n", n=256)).then_inc(raw_in["o"], 16)
                sp.wait_ge(split["q"], E + 1)
                sp.dma_start(raw_vq[:], group(wv, e + 1)).then_inc(raw_in["v"], 16)
                sp.dma_start(raw_vb[:], vrow[bass.ds(e + 1, 1)].rearrange("a b n -> (a b) n").partition_broadcast(P)).then_inc(raw_in["v"], 16)
                sp.wait_ge(split["o"], E + 1 + CR1)
                sp.dma_start(raw_ok[:], group(wk, e + 1)).then_inc(raw_in["k"], 16)
                sp.wait_ge(split["v"], n + 2)
                sp.dma_start(raw_vq[:], group(wa, e + 1)).then_inc(raw_in["q"], 16)

            for half in range(HALVES):
                sp.wait_ge(a_unit, half * (UNITS * HBODIES) + CR1)
                l0_inputs(half)
                if half == 0:
                    sp.dma_start(raw_ok[:], wk[0]).then_inc(raw_in["k"], 16)
                    sp.dma_start(raw_vq[:], wv[0]).then_inc(raw_in["v"], 16)
                    sp.dma_start(raw_vb[:], vrow[0].partition_broadcast(P)).then_inc(raw_in["v"], 16)
                    sp.wait_ge(split["v"], 1)
                    sp.dma_start(raw_vq[:], wa[0]).then_inc(raw_in["q"], 16)
                bias_row(half * 3, 0)
                with sp.Fori(0, LAYERS) as layer:
                    with sp.Fori(0, BODIES - 1) as g:
                        weights(half, layer, g)
                    bias_row(half * 3 + layer + 1, layer + 1)
                    weights(half, layer, BODIES - 1)
                sp.wait_ge(split["k"], half * HBODIES + HBODIES + 1)
                with sp.Fori(HBODIES, STREAM) as e:
                    sp.wait_ge(split["o"], half * STREAM + e + CR1)
                    sp.dma_start(raw_ok[:], group(wb, e).rearrange("p c (a n) -> p (c a) n", n=256)).then_inc(raw_in["o"], 16)
                    sp.wait_ge(split["q"], half * STREAM + e + 1)
                    sp.dma_start(raw_vq[:], group(wa, e + 1)).then_inc(raw_in["q"], 16)

        @block.gpsimd
        def _(pool):
            pool.sem_inc(split["o"], CR1)
            pool.sem_inc(ln_bias, CR1)
            pool.memset(ident[:], 0.0).then_inc(ident_zero, 1)
            pool.memset(minus_half[:], -0.5).then_inc(ident_zero, 1)
            pool.wait_ge(ident_zero, 2)
            pool.affine_select(out=ident[:], in_=ident[:], compare_op=ALU.not_equal, fill=1.0, base=0,
                               pattern=[[-1, P]], channel_multiplier=1).then_inc(ident_ready, 1)
            pool.wait_ge(bn_step, 1)
            pool.tensor_tensor(bnt[:, 1, :], bnt[:, 0, :], minus_half[:, 0:2], ALU.pow).then_inc(bn_rstd, 1)

            def halve(hi_lo, raw, m, count, hi_count):
                wait_apart(pool, raw_in[m], count)
                pool.tensor_copy(hi_lo[0][:], raw if isinstance(raw, bass.AP) else raw[:]).then_inc(hi_part, 1)
                pool.wait_ge(hi_part, hi_count)
                return pool.tensor_tensor(hi_lo[1][:], raw if isinstance(raw, bass.AP) else raw[:], f(hi_lo[0][:]), ALU.subtract)

            def halve_v(done, hi_count):
                halve(wvs, raw_vq, "v", done * 32, hi_count)
                return pool.tensor_tensor(vb[:], raw_vb[:, 0, :], raw_vb[:, 1, :], ALU.subtract)

            halve(wks, raw_ok, "k", 16, 1).then_inc(split["k"], 1)
            halve_v(1, 2).then_inc(split["v"], 1)
            halve(wqs, raw_vq, "q", 16, 3).then_inc(split["q"], 1)
            HI0 = 3
            HI_HALF = 4 * HBODIES + 2 * MBODIES

            def rsqrt(l, p):
                pool.wait_ge(ln_eps, l * 2 + p + 1)
                pool.tensor_tensor(rstd[:], vpe[:], minus_half[:], ALU.pow).then_inc(ln_rstd, 1)

            def add_bias(l, p):
                pool.wait_ge(brow_in, l * 16 + 16)
                for t in range(4 * p, 4 * p + 4):
                    pool.wait_ge(ln_z, l * TILES + t + 1)
                    pool.tensor_tensor(x[:, t, :], x[:, t, :], brow[:], ALU.add).then_inc(ln_bias, 1)

            def attention(half, layer, g, kind):
                e = layer * BODIES + g
                n = pool.snap(half * HBODIES + e)
                E = pool.snap(half * STREAM + e)
                hi0 = pool.snap(half * HI_HALF + e * 4 + HI0)
                l = half * 3 + layer
                if kind == FIRST:
                    rsqrt(l, 1)
                pool.wait_ge(a_unit, n * UNITS + CR1)
                pool.wait_ge(m_unit, half * (MUNITS * MBODIES) + CR1)
                halve(wos, raw_ok[:].rearrange("p (c a) n -> p c (a n)", c=2), "o", E * 16 + 16, hi0 + 1).then_inc(split["o"], 1)
                if kind == FIRST:
                    add_bias(l, 1)
                pool.wait_ge(a_unit, n * UNITS + UNIT["k", 1, 1] + 1 + CR1)
                halve(wks, raw_ok, "k", n * 16 + 32, hi0 + 2).then_inc(split["k"], 1)
                pool.wait_ge(a_free, n * UNITS + UNIT["v", 1, 1] + 1 + CR4)
                halve_v(n + 2, hi0 + 3).then_inc(split["v"], 1)
                pool.wait_ge(a_unit, n * UNITS + UNIT["q", 1, 1] + 1 + CR1)
                halve(wqs, raw_vq, "q", E * 16 + 32, hi0 + 4).then_inc(split["q"], 1)
                if kind == LAST:
                    rsqrt(l + 1, 0)
                    add_bias(l + 1, 0)

            def mlp(half, g, first):
                m = pool.snap(half * MBODIES + g)
                E = pool.snap(half * STREAM + g + HBODIES)
                hi0 = pool.snap(half * HI_HALF + g * 2 + HI0 + 4 * HBODIES)
                if first:
                    rsqrt(half * 3 + 2, 1)
                pool.wait_ge(a_unit, half * (UNITS * HBODIES) + UNITS * HBODIES + CR1)
                pool.wait_ge(m_unit, m * MUNITS + CR1)
                halve(wos, raw_ok[:].rearrange("p (c a) n -> p c (a n)", c=2), "o", E * 16 + 16, hi0 + 1).then_inc(split["o"], 1)
                if first:
                    add_bias(half * 3 + 2, 1)
                pool.wait_ge(m_unit, m * MUNITS + UNITS_M[first].index(("f", 1, 1)) + 1 + CR1)
                halve(wqs, raw_vq, "q", E * 16 + 32, hi0 + 2).then_inc(split["q"], 1)

            with pool.Fori(0, HALVES) as half:
                rsqrt(half * 3, 0)
                add_bias(half * 3, 0)
                with pool.Fori(0, LAYERS) as layer:
                    attention(half, layer, 0, FIRST)
                    with pool.Fori(1, BODIES - 1) as g:
                        attention(half, layer, g, MIDDLE)
                    attention(half, layer, BODIES - 1, LAST)
                mlp(half, 0, True)
                with pool.Fori(1, MBODIES) as g:
                    mlp(half, g, False)

        @block.tensor
        def _(pe):
            pe.sem_inc(a_unit, CR1)
            pe.sem_inc(m_unit, CR1)
            pe.sem_inc(a_T, CR2)
            pe.sem_inc(a_pv, CR1)

            def product(o, lhs, rhs, start, stop):
                pe.matmul(o, lhs[0], rhs[0], start=start, stop=False)
                pe.matmul(o, lhs[0], rhs[1], start=False, stop=False)
                return pe.matmul(o, lhs[1], rhs[0], start=False, stop=stop)

            def parts(pr, *ix):
                return tuple(t[(slice(None), *ix)] for t in pr)

            def proj_half(c, w, h, src, p, s):
                for ch in (2 * s, 2 * s + 1):
                    mm = product(bank(c), parts(w, ch, slice(h * P, h * P + P)),
                                 parts(src, ch, slice(p * 512, p * 512 + 512)), ch == 0, ch == CH - 1)
                return mm

            def v_half(c, p, pair_of, s):
                t = p * 512 + (2 * pair_of + s) * P
                for ch in range(CH):
                    mm = product(bank(c)[:, s * 256:s * 256 + 256], parts(cT, ch, slice(t, t + P)),
                                 parts(wvs, ch, slice(0, 256)), ch == 0, ch == CH - 1)
                return mm

            def out_tile(c, p, t):
                for h in range(2):
                    mm = product(bank(c), parts(oT, p, h, slice(t * P, t * P + P)),
                                 parts(wos, h, slice(0, D)), h == 0, h == 1)
                return mm

            def l0(half):
                pe.wait_ge(m_free, half * (8 * MBODIES) + CR4)
                pe.wait_ge(l0_w, half * 64 + 64)
                seen = set()
                for c, (kind, b, part) in enumerate(L0):
                    needs = {"cT": (l0_c[2 * b % HB], l0_c[(2 * b + 1) % HB]), "pg": (l0_c[b],), "th": (l0_x[b],)}.get(kind, ())
                    for s in needs:
                        if s not in seen:
                            seen.add(s)
                            pe.wait_ge(s, half * 16 + 16)
                    if c >= RING:
                        by = TO_V if L0[c - RING][0] in TO_V else TO_A
                        free, per = (z_free_v, l0_taken(ZUNITS, TO_V)) if by is TO_V else (z_free_a, l0_taken(ZUNITS, TO_A))
                        pe.wait_ge(free, half * per + l0_taken(c - RING, by))
                    nv, na = l0_taken(ZUNITS, TO_V), l0_taken(ZUNITS, TO_A)
                    o = bank(c)
                    if kind == "cT":
                        for t in range(4):
                            mm = pe.transpose(o[:, t * P:t * P + P], c0[:, 4 * b + t, part * P:part * P + P], ident[:])
                    elif kind == "pg":
                        for i in range(2):
                            ch = 2 * part + i
                            for tt in range(2):
                                mm = pe.matmul(o[:, i * 256:i * 256 + 256], c0[:, 2 * b + tt, ch * P:ch * P + P],
                                               wpg[:, tt, :], start=tt == 0, stop=tt == 1)
                    elif kind == "th":
                        for tt in range(2):
                            mm = pe.matmul(o, wth[:, tt, :], x0[:, 2 * b + tt, :], start=tt == 0, stop=tt == 1)
                    elif kind == "M":
                        pe.wait_ge(z_free_v, half * nv + l0_taken(L0.index(("pg", b, 1)), TO_V))
                        for ch in range(CH):
                            mm = pe.matmul(o[:, 0:P], pg[:, ch, 0:P], pg[:, ch, P:2 * P], start=ch == 0, stop=ch == CH - 1)
                    elif kind == "y":
                        pe.wait_ge(z_free_a, half * na + l0_taken(L0.index(("M", b, 0)), TO_A))
                        mm = pe.matmul(o, msb[:], th[:], start=True, stop=True)
                    else:
                        if part == 0:
                            pe.wait_ge(z_free_a, half * na + l0_taken(L0.index(("y", b, 0)), TO_A))
                        mm = pe.matmul(o, www_s[:, part * P:part * P + P], y[:], start=True, stop=True)
                    mm.then_inc(z_unit, 1)

            def prologue(half):
                pe.wait_ge(split["k"], half * HBODIES + 1)
                pe.wait_ge(split["v"], half * HBODIES + 1)
                for c in range(4):
                    pe.wait_ge(ln_affine, half * 24 + c + 1)
                    for s in range(2):
                        mm = proj_half(c, wks, c, cT, 0, s) if c < 2 else v_half(c, 0, c - 2, s)
                    mm.then_inc(pro_unit, 1)

            def norm(l, p, c, free, count):
                pe.wait_ge(ln_z, l * TILES + 4 * p + 4)
                for ch in range(CH):
                    pe.wait_ge(free, count - 3 + ch)
                    for t in range(4):
                        mm = pe.transpose(bank(c + ch)[:, t * P:t * P + P], z[:, t, ch * P:ch * P + P], ident[:])
                    mm.then_inc(ln_T, 1)

            def attention(half, layer, g, kind):
                e = layer * BODIES + g
                n = half * HBODIES + e
                ub = pe.snap(n * UNITS)
                jb = pe.snap(n * ITEMS)
                E = pe.snap(half * STREAM + e)
                l = half * 3 + layer
                if kind == FIRST:
                    pe.wait_ge(pro_free, half * 4 + 4)

                def unit(c, s, turned):
                    what, p, i = UNITS_A[c]
                    if s == 0 or what == "w":
                        pe.wait_ge(a_free, ub + c - RING + 1 + CR4)
                        if turned is not None:
                            pe.wait_ge(ln_affine, turned)
                    if c == 0 and s == 0:
                        pe.wait_ge(split["q"], E + 1)
                        if kind == FIRST:
                            pe.wait_ge(ln_h, l * 8 + 4 + CR2)
                    if (what, p, i, s, kind) == ("q", 1, 0, 0, FIRST):
                        pe.wait_ge(ln_h, l * 8 + 8 + CR2)
                    if (what, i, s) == ("K", 0, 0):
                        pe.wait_ge(split["k"], n + 2)
                    if (what, i, s) == ("V", 0, 0):
                        pe.wait_ge(split["v"], n + 2)
                    if what == "q":
                        mm = proj_half(c, wqs, i, hT, p, s)
                    elif what in "kK":
                        mm = proj_half(c, wks, i, cT, p, s)
                    elif what in "vV":
                        mm = v_half(c, p, i, s)
                    else:
                        if (p, i) == (0, 0):
                            pe.wait_ge(split["o"], E + 1 + CR1)
                        if i in (0, 2):
                            pe.wait_ge(a_o, jb + 4 * p + (3 if i == 0 else 4) + CR1)
                        mm = out_tile(c, p, i)
                    if s == 1:
                        mm.then_inc(a_unit, 1)

                def logits(j):
                    p, h, b = item(j)
                    if b == 0:
                        pe.wait_ge(a_free, ub + UNIT["q", p, h] + 1 + CR4)
                    pe.wait_ge(a_exp, jb + j + CR1)
                    for qt in range(2):
                        q0 = b * 256 + qt * P
                        mm = product(S[:, qt, 0:258], parts(qT, h, slice(q0, q0 + P)), parts(kT, p, h, b), True, True)
                    mm.then_inc(a_logit, 1)

                def turn(j):
                    pe.wait_ge(a_prob, jb + j + 1)
                    pe.wait_ge(a_pt, jb + j + CR1)
                    for tt in range(2):
                        for qt in range(2):
                            mm = pe.transpose(T[:, tt, qt * P:qt * P + P],
                                              probs[:, j % 2, qt, tt * P:tt * P + P], ident[:])
                    mm.then_inc(a_T, 1)

                def values(j):
                    p, h, b = item(j)
                    pe.wait_ge(a_pt, jb + j + 1 + CR1)
                    pe.wait_ge(a_o, jb + j + CR1)
                    for tt in range(2):
                        mm = product(O[:, 0:256], parts(v, p, 2 * b + tt, slice(h * P, h * P + P)),
                                     parts(PT, tt), tt == 0, tt == 1)
                    mm.then_inc(a_pv, 1)

                c_next, turned = 0, {}
                for what, *a in steps(kind):
                    if what == "U":
                        unit(*a, turned.get(a[0]))
                        c_next = a[0] + 1
                    elif what == "L":
                        logits(*a)
                    elif what == "T":
                        turn(*a)
                    elif what == "P":
                        values(*a)
                    else:
                        p = a[0]
                        ln = l if kind == FIRST else l + 1
                        norm(ln, p, c_next, a_free, ub + c_next + CR4)
                        turned = {c_next + ch: ln * 8 + 4 * p + ch + 1 for ch in range(RING)}
                        if c_next + RING > UNITS:
                            raise ValueError("the norm's banks reach into the next body")

            def mlp(half, g, first):
                m = half * MBODIES + g
                E = pe.snap(half * STREAM + g + HBODIES)
                units = UNITS_M[first]
                l = half * 3 + 2
                pe.wait_ge(split["q"], E + 1)
                for c, (what, p, i) in enumerate(units):
                    if first and (what, p, i) == ("w", 0, 0):
                        norm_mlp(l, m)
                    if first and c in range(2, 6):
                        pe.wait_ge(ln_affine, l * 8 + 4 + c - 2 + 1)
                    b_what = (units[c - RING] if c >= RING else ("w", 1, c))[0]
                    if b_what == "w":
                        done = sum(u[0] == "w" for u in units[:c - RING + 1]) if c >= RING else c - 3
                        if not (first and c < 2):
                            pe.wait_ge(m_free, m * 8 + done + CR4)
                        else:
                            pe.wait_ge(a_free, (half + 1) * (UNITS * HBODIES) - 3 + c + CR4)
                    else:
                        pe.wait_ge(m_gelu, m * 4 + sum(u[0] == "f" for u in units[:c - RING + 1]))
                    if what == "f":
                        if first:
                            pe.wait_ge(ln_h, l * 8 + 4 * p + 4 + CR2)
                        for s in range(2):
                            mm = proj_half(c, wqs, i, hT, p, s)
                        mm.then_inc(m_unit, 1)
                    else:
                        if (p, i) == (0, 0):
                            pe.wait_ge(split["o"], E + 1 + CR1)
                        if i == 0:
                            pe.wait_ge(m_act, m * 4 + 2 * p + 2 + CR2)
                        out_tile(c, p, i).then_inc(m_unit, 1)

            def norm_mlp(l, m):
                pe.wait_ge(ln_z, l * TILES + 8)
                for ch in range(CH):
                    if ch < 2:
                        pe.wait_ge(a_free, (m + MBODIES) // MBODIES * (UNITS * HBODIES) - 1 + ch + CR4)
                    else:
                        pe.wait_ge(m_gelu, m * 4 + ch - 1)
                    for t in range(4):
                        mm = pe.transpose(bank(2 + ch)[:, t * P:t * P + P], z[:, t, ch * P:ch * P + P], ident[:])
                    mm.then_inc(ln_T, 1)

            pe.wait_ge(ident_ready, 1)
            with pe.Fori(0, HALVES) as half:
                l0(half)
                pe.wait_ge(z_free_v, (half + 1) * l0_taken(ZUNITS, TO_V))
                norm(half * 3, 0, 0, z_free_a, (half + 1) * l0_taken(ZUNITS, TO_A))
                prologue(half)
                with pe.Fori(0, LAYERS) as layer:
                    attention(half, layer, 0, FIRST)
                    with pe.Fori(1, BODIES - 1) as g:
                        attention(half, layer, g, MIDDLE)
                    attention(half, layer, BODIES - 1, LAST)
                mlp(half, 0, True)
                with pe.Fori(1, MBODIES) as g:
                    mlp(half, g, False)

        @block.scalar
        def _(act):
            act.sem_inc(a_exp, CR1)
            act.sem_inc(stored, CR1)
            act.wait_ge(consts_in, 16 * 5)
            act.activation(bkx[0][:], hc[:, 2, :], ACT.Copy).then_inc(bk_hi, 1)
            ZU_A, ZU_V = l0_taken(ZUNITS, TO_A), l0_taken(ZUNITS, TO_V)

            def l0(half):
                for c, (kind, b, part) in enumerate(L0):
                    o = bank(c)
                    if kind == "pg":
                        continue
                    act.wait_ge(z_unit, half * ZUNITS + c + 1)
                    if kind == "cT":
                        act.activation(cT[0][:, part, b * 512:b * 512 + 512], o, ACT.Copy).then_inc(z_hi, 1)
                    elif kind == "th":
                        act.activation(th[:], o, ACT.Identity, bias=thb_s[:, 0:1]).then_inc(z_free_a, 1)
                    elif kind == "M":
                        act.activation(msb[:], o[:, 0:P], ACT.Copy, scale=1.0 / D).then_inc(z_free_a, 1)
                    elif kind == "y":
                        act.activation(y[:], o, ACT.Copy).then_inc(z_free_a, 1)
                    else:
                        k = 2 * b + part
                        if k == 0:
                            act.wait_ge(bn_ready, 1)
                        act.wait_ge(z_x, half * TILES + k - 1 + CR2)
                        act.activation(tmp[:, part, :], o, ACT.Identity, bias=bns[:, 1, part:part + 1],
                                       scale=bns[:, 0, part:part + 1]).then_inc(z_free_a, 1)

            def kv_hi(c, p, h, waits, b, count, hi, v32, col):
                if h < 2:
                    act.wait_ge(waits, count)
                    act.activation(kview(0, p, h), two(bank(c)), ACT.Identity, bias=col).then_inc(hi, 1)
                else:
                    act.wait_ge(v32, b)
                    act.activation(vview(0, p, h - 2), two(tmp[:, h - 2, :]), ACT.Copy).then_inc(hi, 1)

            def norm(l, li, p, c):
                for ch in range(CH):
                    k = 4 * p + ch
                    wait_apart(act, ln_T, l * 8 + k + 1)
                    wait_apart(act, ln_h, l * 8 + k - 1 + CR2)
                    act.activation(aff[:, k % 2, :], bank(c + ch), ACT.Identity, bias=lnc[:, 1, bass.ds(li * CH + ch, 1)],
                                   scale=lnc[:, 0, bass.ds(li * CH + ch, 1)]).then_inc(ln_affine, 1)

            def attention(half, layer, g, kind):
                e = layer * BODIES + g
                n = half * HBODIES + e
                ub = act.snap(n * UNITS)
                jb = act.snap(n * ITEMS)
                vb4 = act.snap(n * 4)
                head = act.snap(e * 2)

                def unit_hi(c):
                    what, p, i = UNITS_A[c]
                    if what == "q":
                        wait_apart(act, a_unit, ub + c + 1 + CR1)
                        act.activation(qslot(0, i), bank(c), ACT.Identity,
                                       bias=hc[:, 0, bass.ds(head + i, 1)]).then_inc(a_hi, 1)
                    elif what in "kK":
                        wait_apart(act, a_unit, ub + c + 1 + CR1)
                        act.activation(kview(0, p, i), two(bank(c)), ACT.Identity,
                                       bias=hc[:, 1, bass.ds(head + i + 2 * (what == "K"), 1)]).then_inc(a_hi, 1)
                    elif what in "vV":
                        act.wait_ge(a_v32, vb4 + V_UNITS.index(c) + 1)
                        act.activation(vview(0, p, i), two(tmp[:, i, :]), ACT.Copy).then_inc(a_hi, 1)

                def softmax(j):
                    act.wait_ge(a_max, jb + j + 1)
                    act.wait_ge(a_T, jb + j - 1 + CR2)
                    for qt in range(2):
                        ins = act.activation(probs[:, j % 2, qt, 0:257], S[:, qt, 0:257], ACT.Exp,
                                             bias=nm[:, j % 2, qt:qt + 1], scale=SCALE,
                                             accum_out=sums[:, j % 2, qt:qt + 1])
                    ins.then_inc(a_exp, 1)

                def turned_hi(j):
                    act.wait_ge(a_T, jb + j + 1 + CR2)
                    act.wait_ge(a_pv, jb + j + CR1)
                    act.activation(PT[0][:], T[:], ACT.Copy).then_inc(a_pthi, 1)

                def o_hi(j):
                    p, h, b = item(j)
                    wait_apart(act, a_pv, jb + j + 1 + CR1)
                    act.activation(oT[0][:, p, h, b * 256:b * 256 + 256], O[:, 0:256], ACT.Identity,
                                   bias=hc[:, 3, bass.ds(head + h, 1)]).then_inc(a_ohi, 1)

                c_next = 0
                for what, *a in steps(kind):
                    if what == "U":
                        c_next = a[0] + 1
                        if a[1] == 1:
                            unit_hi(a[0])
                    elif what == "L":
                        if a[0] == 0:
                            softmax(0)
                    elif what == "T":
                        turned_hi(*a)
                        if a[0] + 1 < ITEMS:
                            softmax(a[0] + 1)
                    elif what == "P":
                        o_hi(*a)
                    elif kind == FIRST:
                        norm(half * 3 + layer, layer, a[0], c_next)
                    else:
                        norm(half * 3 + layer + 1, layer + 1, a[0], c_next)

            def mlp(half, g, first):
                m = half * MBODIES + g
                done = 0
                for c, (what, p, i) in enumerate(UNITS_M[first]):
                    if first and c == 2:
                        norm(half * 3 + 2, 2, 1, 2)
                    if what == "f":
                        wait_apart(act, m_unit, m * MUNITS + c + 1 + CR1)
                        wait_apart(act, m_act, m * 4 + done - 1 + CR2)
                        act.activation(tmp[:, i, :], bank(c), ACT.Gelu,
                                       bias=f1c[:, bass.ds(g * 2 + i, 1)]).then_inc(m_gelu, 1)
                        done += 1

            with act.Fori(0, HALVES) as half:
                l0(half)
                norm(half * 3, 0, 0, 0)
                act.wait_ge(z_x, half * TILES + TILES + CR2)
                for c in range(4):
                    kv_hi(c, 0, c, pro_unit, half * 2 + c - 1, half * 4 + c + 1, pro_hi, pro_v32, hc[:, 1, c % 2:c % 2 + 1])
                with act.Fori(0, LAYERS) as layer:
                    attention(half, layer, 0, FIRST)
                    with act.Fori(1, BODIES - 1) as g:
                        attention(half, layer, g, MIDDLE)
                    attention(half, layer, BODIES - 1, LAST)
                mlp(half, 0, True)
                with act.Fori(1, MBODIES) as g:
                    mlp(half, g, False)
                act.wait_ge(m_free, half * (8 * MBODIES) + 8 * MBODIES + CR4)
                for p in range(2):
                    act.dma_start(out[bass.ds(half * 2 + p, 1)].rearrange("a t p n -> p (a t) n"),
                                  x[:, 4 * p:4 * p + 4, :]).then_inc(stored, 16)
            act.wait_ge(stored, HALVES * 32 + CR1)

        @block.vector
        def _(dve):
            for s, k in ((m_free, CR4), (a_free, CR4), (z_x, CR2), (ln_h, CR2), (a_pt, CR1), (a_o, CR1), (m_act, CR2)):
                dve.sem_inc(s, k)
            dve.wait_ge(consts_in, 16 * 5)
            dve.tensor_scalar(bnt[:, 0, :], bnc[:, 3, :], EPS, None, ALU.add).then_inc(bn_step, 1)
            dve.wait_ge(bn_rstd, 1)
            dve.tensor_tensor(bns[:, 0, :], bnc[:, 0, :], bnt[:, 1, :], ALU.mult).then_inc(bn_step, 1)
            dve.tensor_tensor(bnt[:, 2, :], bnc[:, 4, :], bnc[:, 2, :], ALU.subtract).then_inc(bn_step, 1)
            dve.wait_ge(bn_step, 3)
            dve.tensor_tensor(bnt[:, 2, :], bnt[:, 2, :], bns[:, 0, :], ALU.mult).then_inc(bn_step, 1)
            dve.wait_ge(bn_step, 4)
            dve.tensor_tensor(bns[:, 1, :], bnt[:, 2, :], bnc[:, 1, :], ALU.add).then_inc(bn_ready, 1)
            dve.wait_ge(bk_hi, 1)
            dve.tensor_tensor(bkx[1][:], hc[:, 2, :], f(bkx[0][:]), ALU.subtract).then_inc(bk_lo, 1)
            dve.wait_ge(bk_lo, 1)

            def tile_stats(p, t):
                dve.bn_stats(stats[:, t, :], x[:, 4 * p + t, :]).then_inc(ln_stats, 1)

            def moments(l, p):
                for t in range(4):
                    wait_apart(dve, ln_stats, l * 8 + 4 * p + t + 1)
                    dve.bn_aggr(mv[:, t, :], stats[:, t, :]).then_inc(ln_mv, 1)
                dve.wait_ge(ln_mv, l * 8 + 4 * p + 4)
                dve.tensor_scalar(vpe[:], mv[:, :, 1], EPS, None, ALU.add).then_inc(ln_eps, 1)

            def normalise(l, p):
                dve.wait_ge(ln_rstd, l * 2 + p + 1)
                for t in range(4):
                    dve.tensor_scalar(z[:, t, :], x[:, 4 * p + t, :], mv[:, t, 0:1], rstd[:, t:t + 1],
                                      ALU.subtract, ALU.mult).then_inc(ln_z, 1)

            def l0(half):
                his = 0
                for c, (kind, b, part) in enumerate(L0):
                    o = bank(c)
                    if kind == "cT":
                        his += 1
                        dve.wait_ge(z_hi, half * 8 + his)
                        to = slice(b * 512, b * 512 + 512)
                        dve.tensor_tensor(cT[1][:, part, to], o, f(cT[0][:, part, to]), ALU.subtract).then_inc(z_free_v, 1)
                    elif kind == "pg":
                        dve.wait_ge(z_unit, half * ZUNITS + c + 1)
                        dve.tensor_tensor(pg[:, 2 * part:2 * part + 2, :], two(o),
                                          pgb_s[:].unsqueeze(1).to_broadcast([P, 2, 256]), ALU.add).then_inc(z_free_v, 1)
                    elif kind == "wy":
                        k = 2 * b + part
                        if k == 0:
                            dve.wait_ge(stored, half * 32 + CR1)
                        dve.wait_ge(z_free_a, half * l0_taken(ZUNITS, TO_A) + l0_taken(c, TO_A))
                        dve.tensor_tensor(x[:, k, :], tmp[:, part, :], x0[:, k, :], ALU.add).then_inc(z_x, 1)
                        if k < 4:
                            dve.wait_ge(z_x, half * TILES + k + 1 + CR2)
                            tile_stats(0, k)
                        if k == 3:
                            moments(half * 3, 0)
                        if k == 4:
                            normalise(half * 3, 0)

            def k_lo(c, p, h, hi, hi_count, col, bk_col):
                for part in range(2):
                    dve.tensor_copy(kT[part][:, p, h, :, 256:258],
                                    bk_col(f(bkx[part][:])).unsqueeze(2).to_broadcast([P, 2, 2]))
                dve.wait_ge(hi, hi_count)
                return dve.scalar_tensor_tensor(out=kview(1, p, h), in0=two(bank(c)), scalar=col,
                                                in1=f(kview(0, p, h)), op0=ALU.add, op1=ALU.subtract)

            def v_lo(c, p, i, v32, v_count, hi, hi_count):
                dve.tensor_tensor(two(tmp[:, i, :]), two(bank(c)), vb[:].unsqueeze(1).to_broadcast([P, 2, 256]),
                                  ALU.add).then_inc(v32, 1)
                dve.wait_ge(v32, v_count)
                dve.wait_ge(hi, hi_count)
                return dve.tensor_tensor(vview(1, p, i), two(tmp[:, i, :]), f(vview(0, p, i)), ALU.subtract)

            def prologue(half):
                dve.wait_ge(z_x, half * TILES + TILES + CR2)
                for c in range(4):
                    dve.wait_ge(pro_unit, half * 4 + c + 1)
                    if c < 2:
                        ins = k_lo(c, 0, c, pro_hi, half * 4 + c + 1, hc[:, 1, c:c + 1], lambda t, c=c: t[:, c:c + 1])
                    else:
                        ins = v_lo(c, 0, c - 2, pro_v32, half * 2 + c - 1, pro_hi, half * 4 + c + 1)
                    ins.then_inc(pro_free, 1)

            def spread(l, p):
                for ch in range(CH):
                    k = p * CH + ch
                    to = slice(p * 512, p * 512 + 512)
                    dve.wait_ge(ln_affine, l * 8 + k + 1)
                    dve.tensor_copy(hT[0][:, ch, to], aff[:, k % 2, :]).then_inc(ln_hi, 1)
                    dve.wait_ge(ln_hi, l * 8 + k + 1)
                    dve.tensor_tensor(hT[1][:, ch, to], aff[:, k % 2, :], f(hT[0][:, ch, to]), ALU.subtract).then_inc(ln_h, 1)

            def attention(half, layer, g, kind):
                e = layer * BODIES + g
                n = half * HBODIES + e
                ub = dve.snap(n * UNITS)
                jb = dve.snap(n * ITEMS)
                hb = dve.snap(n * len(HI_UNITS))
                vb4 = dve.snap(n * 4)
                head = dve.snap(e * 2)
                l = half * 3 + layer

                def unit_lo(c):
                    what, p, i = UNITS_A[c]
                    hi_count = hb + HI_UNITS.index(c) + 1 if c in HI_UNITS else None
                    if what == "q":
                        dve.wait_ge(a_hi, hi_count)
                        ins = dve.scalar_tensor_tensor(out=qslot(1, i), in0=bank(c), scalar=hc[:, 0, bass.ds(head + i, 1)],
                                                       in1=f(qslot(0, i)), op0=ALU.add, op1=ALU.subtract)
                    elif what in "kK":
                        at = head + i + 2 * (what == "K")
                        dve.wait_ge(a_unit, ub + c + 1 + CR1)
                        ins = k_lo(c, p, i, a_hi, hi_count, hc[:, 1, bass.ds(at, 1)], lambda t: t[:, bass.ds(at, 1)])
                    elif what in "vV":
                        if i == 0:
                            dve.wait_ge(split["v"], n + 1 + (what == "V"))
                        dve.wait_ge(a_unit, ub + c + 1 + CR1)
                        ins = v_lo(c, p, i, a_v32, vb4 + V_UNITS.index(c) + 1, a_hi, hi_count)
                    else:
                        if kind == FIRST and i == 0:
                            dve.wait_ge(ln_bias, l * 8 + 4 * p + 4 + CR1)
                        t = 4 * p + i
                        dve.wait_ge(a_unit, ub + c + 1 + CR1)
                        ins = dve.tensor_tensor(x[:, t, :], x[:, t, :], bank(c), ALU.add)
                    ins.then_inc(a_free, 1)

                def max_of(j):
                    dve.wait_ge(a_logit, jb + j + 1)
                    dve.tensor_reduce(mx[:, j % 2, :], S[:, :, 0:257], AX.X, ALU.max).then_inc(a_rawmax, 1)
                    dve.wait_ge(a_rawmax, jb + j + 1)
                    dve.tensor_scalar(nm[:, j % 2, :], mx[:, j % 2, :], -SCALE, None, ALU.mult).then_inc(a_max, 1)

                def divide(j):
                    r = j % 2
                    dve.wait_ge(a_exp, jb + j + 1 + CR1)
                    dve.reciprocal(rs[:, r, :], sums[:, r, :]).then_inc(a_rcp, 1)
                    dve.wait_ge(a_rcp, jb + j + 1)
                    for qt in range(2):
                        ins = dve.tensor_scalar(probs[:, r, qt, 0:256], probs[:, r, qt, 0:256], rs[:, r, qt:qt + 1], None, ALU.mult)
                    ins.then_inc(a_prob, 1)

                def turned_lo(j):
                    dve.wait_ge(a_pthi, jb + j + 1)
                    dve.tensor_tensor(PT[1][:], T[:], f(PT[0][:]), ALU.subtract).then_inc(a_pt, 1)

                def o_lo(j):
                    p, h, b = item(j)
                    to = slice(b * 256, b * 256 + 256)
                    dve.wait_ge(a_ohi, jb + j + 1)
                    dve.scalar_tensor_tensor(out=oT[1][:, p, h, to], in0=O[:, 0:256], scalar=hc[:, 3, bass.ds(head + h, 1)],
                                             in1=f(oT[0][:, p, h, to]), op0=ALU.add, op1=ALU.subtract).then_inc(a_o, 1)

                if kind == FIRST:
                    dve.wait_ge(z_x, half * TILES + TILES + CR2)
                    dve.wait_ge(a_free, ub + CR4)
                    for t in range(4):
                        tile_stats(1, t)
                    moments(l, 1)
                for what, *a in steps(kind):
                    if what == "U":
                        c, s = a
                        if s == 1:
                            unit_lo(c)
                        if kind == FIRST and a == [UNIT["q", 0, 1], 1]:
                            normalise(l, 1)
                        if kind == LAST and UNITS_A[c][:2] == ("w", 0):
                            dve.wait_ge(a_free, ub + c + 1 + CR4)
                            tile_stats(0, UNITS_A[c][2])
                        if kind == LAST and c == W0_END:
                            moments(l + 1, 0)
                        if kind == LAST and a == [W0_END + 1, 0]:
                            normalise(l + 1, 0)
                    elif what == "L":
                        max_of(*a)
                        if a[0] == 0:
                            divide(0)
                    elif what == "T":
                        turned_lo(*a)
                        if a[0] + 1 < ITEMS:
                            divide(a[0] + 1)
                    elif what == "P":
                        o_lo(*a)
                    else:
                        spread(l if kind == FIRST else l + 1, a[0])

            def mlp(half, g, first):
                m = half * MBODIES + g
                l = half * 3 + 2
                fs = ws = 0
                if first:
                    dve.wait_ge(a_free, (half + 1) * (UNITS * HBODIES) + CR4)
                    for t in range(4):
                        tile_stats(1, t)
                    moments(l, 1)
                    normalise(l, 1)
                for c, (what, p, i) in enumerate(UNITS_M[first]):
                    if first and c == 2:
                        spread(l, 1)
                    if what == "f":
                        fs += 1
                        dve.wait_ge(m_gelu, m * 4 + fs)
                        dve.tensor_copy(oT[0][:, p, i, :], tmp[:, i, :]).then_inc(m_hi, 1)
                        dve.wait_ge(m_hi, m * 4 + fs)
                        dve.tensor_tensor(oT[1][:, p, i, :], tmp[:, i, :], f(oT[0][:, p, i, :]), ALU.subtract).then_inc(m_act, 1)
                    else:
                        if first and i == 0:
                            dve.wait_ge(ln_bias, l * 8 + 4 * p + 4 + CR1)
                        t = 4 * p + i
                        dve.wait_ge(m_unit, m * MUNITS + c + 1 + CR1)
                        dve.tensor_tensor(x[:, t, :], x[:, t, :], bank(c), ALU.add).then_inc(m_free, 1)

            with dve.Fori(0, HALVES) as half:
                l0(half)
                spread(half * 3, 0)
                prologue(half)
                with dve.Fori(0, LAYERS) as layer:
                    attention(half, layer, 0, FIRST)
                    with dve.Fori(1, BODIES - 1) as g:
                        attention(half, layer, g, MIDDLE)
                    attention(half, layer, BODIES - 1, LAST)
                mlp(half, 0, True)
                with dve.Fori(1, MBODIES) as g:
                    mlp(half, g, False)


def _laid_out(i):
    a = {k.replace("L0_xattn_", "").replace("L1_xattn_", "L1"): np.ascontiguousarray(v) for k, v in i.items()}

    def col(vec):
        return vec.reshape(-1, P).T

    def heads(*vecs):
        c = col(np.concatenate([v.reshape(-1) for v in vecs]))
        return np.concatenate([c, c[:, :2]], 1)

    def in_groups(w):
        return w.reshape(CH, P, -1, 256).transpose(2, 1, 0, 3)

    def out_groups(w):
        return w.reshape(-1, 2, P, D).transpose(0, 2, 1, 3)

    def both(name):
        return [a[f"L1{name}1"], a[f"L1{name}2"]]

    q = np.concatenate([in_groups(w) for w in both("wq")] + [in_groups(a["L1w_fc1"])])
    k, v = (np.concatenate([in_groups(w) for w in both(s)]) for s in ("wk", "wv"))
    vr = np.stack([np.concatenate([r.reshape(-1) for r in both(s)]).reshape(HBODIES, 256) for s in ("bv", "bias_v")], 1)
    tiles = (HALVES * 2, 4, P, D)
    lns = [[a[f"L1ln{n}_{s}"] for n in ("1", "2", "_mlp")] for s in ("scale", "offset")]
    return {
        "x_in": a["x"].reshape(tiles),
        "ctx_in": a["ctx_2048"].reshape(tiles),
        "thw": a["theta_w"].T.reshape(2, P, CI).transpose(1, 0, 2),
        "thb": col(a["theta_b"]),
        "pgw": np.concatenate([a["phi_w"].T, a["g_w"].T], 1).reshape(2, P, 2 * CI).transpose(1, 0, 2),
        "pgb": np.concatenate([a["phi_b"], a["g_b"]]),
        "www": a["w_w"].T,
        "bncol": np.stack([col(a[s]) for s in ("bn_gamma", "bn_beta", "bn_mean", "bn_var", "w_b")], 1),
        "wa": np.concatenate([q, q[:1]]),
        "wk": np.concatenate([k, k[:1]]),
        "wv": np.concatenate([v, v[:1]]),
        "wb": np.concatenate([out_groups(w) for w in both("wo")] + [out_groups(a["L1w_fc2"])]),
        "hcol": np.stack([heads(*both(s)) for s in ("bq", "bk", "bias_k", "bias_v")], 1),
        "vrow": np.concatenate([vr, vr[:1]]),
        "lncol": np.stack([np.concatenate([col(x) for x in r], 1) for r in lns], 1),
        "f1col": col(a["L1b_fc1"]),
        "orow": np.stack([*both("bo"), a["L1b_fc2"]]),
    }


def kernel(**inputs):
    import concourse.bacc as bacc
    from concourse.bass_utils import run_bass_kernel_spmd

    nc = bacc.Bacc("TRN2", target_bir_lowering=False, num_devices=1)
    arrays = {k: np.ascontiguousarray(v) for k, v in _laid_out(inputs).items()}
    args = [nc.dram_tensor(k, v.shape, mybir.dt.from_np(v.dtype), kind="ExternalInput").ap() for k, v in arrays.items()]
    out = nc.dram_tensor("out", (HALVES * 2, 4, P, D), F32, kind="ExternalOutput").ap()
    bass_xattn(nc, *args, out)
    r = run_bass_kernel_spmd(nc, [arrays], core_ids=[0])
    return r.results[0]["out"].reshape(B, TOK, D)
```

```python
from contextlib import ExitStack

import numpy as np
import concourse.bass as bass
from concourse import mybir

F32 = mybir.dt.float32
F32R = mybir.dt.float32r
ALU = mybir.AluOpType
ACT = mybir.ActivationFunctionType
AX = mybir.AxisListType

B, TOK, D = 8, 256, 512
CI = 128
H, K, F = 16, 128, 2048
P = 128
EPS = 1e-5
HALVES = 2
HB = B // HALVES
TILES = HB * TOK // P
CH = D // P
LAYERS = 2
BODIES = H // 2
MBODIES = F // 256
HBODIES = LAYERS * BODIES
STREAM = HBODIES + MBODIES
NORMS = LAYERS + 1
TURNS = 2 * CH
SCALE = float(1.0 / np.sqrt(np.float32(K)))

ITEMS = 8
RING = 4
CR4, CR2, CR1 = 4, 2, 1

FIRST, MIDDLE, LAST, FINAL = range(4)

UNITS_A = [("q", 0, 0), ("q", 0, 1), ("k", 1, 0), ("k", 1, 1), ("v", 1, 0), ("v", 1, 1), ("q", 1, 0), ("q", 1, 1),
           ("w", 0, 0), ("w", 0, 1), ("K", 0, 0), ("w", 0, 2), ("w", 0, 3), ("K", 0, 1), ("V", 0, 0), ("V", 0, 1),
           ("w", 1, 0), ("w", 1, 1), ("w", 1, 2), ("w", 1, 3)]


def units_of(kind):
    return [u for u in UNITS_A if kind != FINAL or u[0] not in "KV"]


def per_body(what, kind=MIDDLE):
    return sum(u[0] in what for u in units_of(kind))


def before(half, e, what):
    return half * ((HBODIES - 1) * per_body(what) + per_body(what, FINAL)) + e * per_body(what)


def nth(units, c, what):
    return sum(u[0] in what for u in units[:c + 1])


ALL, OPERANDS, VS = "qkvKVw", "qkvKV", "vV"

UNITS_M = {first: [("f", 0, 0), ("f", 0, 1)] + rest for first, rest in (
    (True, [("w", 0, 0), ("w", 0, 1), ("w", 0, 2), ("f", 1, 0), ("f", 1, 1), ("w", 0, 3)] +
     [("w", 1, t) for t in range(4)]),
    (False, [("f", 1, 0), ("f", 1, 1)] + [("w", p, t) for p in range(2) for t in range(4)]))}
MUNITS = 12
MTILES = TILES


ORDER = {
    FIRST: "uuuu L0 uuu L1 T0 u Z A0 A1 u A2 P0 A3 u L2 T1 uu P1 u L3 T2 uu P2 u L4 T3 uu P3 u "
           "L5 T4 uu P4 u L6 T5 uu P5 L7 T6 uu P6 u T7 uu P7 uuu",
    MIDDLE: "uuuu L0 uuu L1 T0 uu P0 u L2 T1 uu P1 u L3 T2 uu P2 u L4 T3 uu P3 u "
            "L5 T4 uu P4 u L6 T5 uu P5 L7 T6 uu P6 u T7 uu P7 uuu",
    LAST: "uuuu L0 uuu L1 T0 uu P0 u L2 T1 uu P1 u L3 T2 uu P2 u L4 T3 uu P3 u "
          "L5 T4 uu P4 u L6 T5 uu P5 L7 T6 uu P6 T7 Z A0 A1 u A2 uu A3 P7 uuu",
    FINAL: "uuuu L0 uuu L1 T0 uu P0 u L2 T1 uu P1 L3 T2 uu P2 u L4 T3 uu P3 "
           "L5 T4 uu P4 u L6 T5 P5 L7 T6 Z A0 P6 A1 T7 A2 u A3 P7 uuu",
}


def steps(kind):
    halves = [(c, s) for c, u in enumerate(units_of(kind)) for s in ((1,) if u[0] == "w" else (0, 1))]
    normed = int(kind == FIRST)
    out = []
    for word in ORDER[kind].split():
        if word[0] == "u":
            for _ in word:
                out.append(("U", *halves.pop(0)))
        elif word == "Z":
            out.append(("Z", normed))
        elif word[0] == "A":
            out.append(("A", normed, int(word[1:])))
        else:
            out.append((word[0], int(word[1:])))
    assert not halves
    return out


def norm_units(kind):
    after = steps(kind)
    after = after[[a[0] for a in after].index("Z"):]
    begun = [a[1] for a in after if a[0] == "U" and (a[2] == 0 or units_of(kind)[a[1]][0] == "w")]
    assert len({c % RING for c in begun[:CH]}) == CH
    return begun[:CH]


def item(j):
    return j // 4, (j % 4) // 2, j % 2


ZUNITS = 2 * CH + 7 * HB
TO_V, TO_A = ("cT", "pg"), ("th", "M", "WM", "wy")


def l0_units():
    units = [("pg", 0, 0), ("pg", 0, 1), ("th", 0, 0)]
    turns = [("cT", p, c) for p in range(2) for c in range(CH)]
    for b in range(HB):
        nxt = b + 1 < HB
        units += [("M", b, 0), ("pg", b + 1, 0) if nxt else turns.pop(0), ("WM", b, 0)]
        units += [("pg", b + 1, 1)] if nxt else []
        units += [turns.pop(0), ("wy", b, 0), ("wy", b, 1)]
        units += [turns.pop(0), ("th", b + 1, 0)] if nxt else []
    return units


L0 = l0_units()
assert len(L0) == ZUNITS and ZUNITS % RING == 0


def l0_taken(c, by):
    return sum(u[0] in by for u in L0[:c + 1])


def bass_xattn(nc, x_in, ctx_in, thw, thb, pgw, pgb, www, bncol, wa, wk, wv, wb, hcol, vrow,
               lncol, f1col, orow, out):
    ctx = ExitStack()
    with ctx:
        def sb(name, shape, dt=F32):
            return ctx.enter_context(nc.sbuf_tensor(name, [P, *shape], dt))

        def pair(name, shape):
            return sb(name + "_hi", shape, F32R), sb(name + "_lo", shape, F32R)

        def sem(name):
            return ctx.enter_context(nc.semaphore(name))

        def f(ap):
            return ap.bitcast(F32)

        def over(names_shapes, first, size):
            at, made = first, []
            for name, shape in names_shapes:
                made.append(nc.alloc_sbuf_tensor_at(name, [P, *shape], F32, offset=at))
                at += 4 * int(np.prod(shape))
            assert at <= first + size
            return made

        def next_address():
            return -(-nc.sbuf_base // 32) * 32

        x = sb("x", [TILES, D])
        hT = pair("hT", [CH, HB * TOK])
        cT = pair("cT", [CH, HB * TOK])
        wqs = pair("wqs", [CH, 256])
        wks = pair("wks", [CH, 256])
        wvs = pair("wvs", [CH, 256])
        wos = pair("wos", [2, D])
        raw_ok = sb("raw_ok", [CH, 256])
        raw_vq = sb("raw_vq", [CH, 256])
        z = sb("z", [4, D])
        aff = sb("aff", [2, 512])
        raw_vb = sb("raw_vb", [2, 256])
        vb = sb("vb", [256])
        PT = pair("PT", [2, 256])
        probs = sb("probs", [2, 2, 258])
        tmp = sb("tmp", [2, 512])
        ident = sb("ident", [P])
        hc = sb("hc", [4, 34])
        bkx = pair("bkx", [34])
        lnc = sb("lnc", [2, 3 * CH])
        f1c = sb("f1c", [F // P])
        thb_s = sb("thb_s", [1])
        brow = sb("brow", [D])
        bnc = sb("bnc", [5, 2])
        bns = sb("bns", [2, 2])
        bnt = sb("bnt", [3, 2])
        minus_half = sb("minus_half", [4])
        stats = sb("stats", [4, 6])
        mv = sb("mv", [4, 2])
        vpe = sb("vpe", [4])
        rstd = sb("rstd", [4])
        mx = sb("mx", [2, 2])
        nm = sb("nm", [2, 2])
        sums = sb("sums", [2, 2])
        rs = sb("rs", [2, 2])
        at = next_address()
        qT = pair("qT", [2, 512])
        wth, wpg, www_s, pgb_s = over([("wth", [2, CI]), ("wpg", [2, 2 * CI]), ("www_s", [TOK]),
                                       ("pgb_s", [2 * CI])], at, nc.sbuf_base - at)
        at = next_address()
        kT = pair("kT", [2, 2, 2, 258])
        v = pair("v", [2, 4, 256])
        x0, c0 = over([("x0", [TILES, D]), ("c0", [TILES, D])], at, nc.sbuf_base - at)
        at = next_address()
        oT = pair("oT", [2, 2, 512])
        pg, th, wm, msb = over([("pg", [4, 256]), ("th", [D]), ("wm", [TOK]), ("msb", [P])], at, nc.sbuf_base - at)

        U = ctx.enter_context(nc.psum_tensor("U", [P, RING, 512], F32))
        S = ctx.enter_context(nc.psum_tensor("S", [P, 2, 512], F32))
        T = ctx.enter_context(nc.psum_tensor("T", [P, 2, 256], F32))
        O = ctx.enter_context(nc.psum_tensor("O", [P, 512], F32))

        consts_in, stored = sem("consts_in"), sem("stored")
        l0_c, l0_x = ([sem(f"l0_{m}{b}") for b in range(HB)] for m in "cx")
        l0_w = sem("l0_w")
        ident_zero, ident_ready = sem("ident_zero"), sem("ident_ready")
        bn_step, bn_rstd, bn_ready = sem("bn_step"), sem("bn_rstd"), sem("bn_ready")
        bk_hi, bk_lo = sem("bk_hi"), sem("bk_lo")
        raw_in = {m: sem("raw_in_" + m) for m in "qkvo"}
        split = {m: sem("split_" + m) for m in "qkvo"}
        hi_part = sem("hi_part")
        z_unit, z_free_v, z_free_a, z_hi, z_x = (sem("z_" + s) for s in ("unit", "free_v", "free_a", "hi", "x"))
        pro_unit, pro_hi, pro_v32, pro_free = (sem("pro_" + s) for s in ("unit", "hi", "v32", "free"))
        ln_stats, ln_mv, ln_eps, ln_rstd, ln_z = (sem("ln_" + s) for s in ("stats", "mv", "eps", "rstd", "z"))
        ln_T, ln_affine, ln_hi, ln_h, ln_bias = (sem("ln_" + s) for s in ("T", "affine", "hi", "h", "bias"))
        brow_in, apart = sem("brow_in"), sem("apart")
        a_unit, a_free, a_hi, a_v32 = (sem("a_" + s) for s in ("unit", "free", "hi", "v32"))
        a_logit, a_T, a_pv = (sem("a_" + s) for s in ("logit", "T", "pv"))
        a_rawmax, a_max, a_exp, a_rcp, a_prob = (sem("a_" + s) for s in ("rawmax", "max", "exp", "rcp", "prob"))
        a_pthi, a_pt, a_ohi, a_o = (sem("a_" + s) for s in ("pthi", "pt", "ohi", "o"))
        m_unit, m_gelu, m_hi, m_act, m_free = (sem("m_" + s) for s in ("unit", "gelu", "hi", "act", "free"))

        block = ctx.enter_context(nc.Block())

        def bank(c):
            return U[:, c % RING, :]

        def qslot(part, h):
            return qT[part][:, h, :]

        def kview(part, p, h):
            return kT[part][:, p, h, :, 0:256]

        def vview(part, p, pair_of):
            return v[part][:, p, 2 * pair_of:2 * pair_of + 2, :]

        def two(ap):
            return ap.rearrange("p (a n) -> p a n", a=2)

        def kept(eng, value):
            return value if isinstance(value, int) else eng.snap(value)

        def wait_apart(eng, sem, value):
            eng.wait_ge(sem, value)
            eng.sem_inc(apart, 1)

        @block.sync
        def _(sp):
            def group(w, e):
                return w[bass.ds(e, 1)].rearrange("a p c n -> (a p) c n")

            def l0_inputs(half):
                for src, dst in ((pgw, wpg), (thw, wth), (www, www_s)):
                    sp.dma_start(dst[:], src).then_inc(l0_w, 16)
                sp.dma_start(pgb_s[:], pgb.partition_broadcast(P)).then_inc(l0_w, 16)
                for b in range(HB):
                    for src, dst, s in ((ctx_in, c0, l0_c), (x_in, x0, l0_x)):
                        sp.dma_start(dst[:, 2 * b:2 * b + 2, :],
                                     src[half * 2 + b // 2, 2 * (b % 2):2 * (b % 2) + 2].rearrange("t p n -> p t n")).then_inc(s[b], 16)
                    if (half, b) == (0, 0):
                        for dst, src in ((thb_s, thb), (bnc, bncol), (hc, hcol), (lnc, lncol), (f1c, f1col)):
                            sp.dma_start(dst[:], src).then_inc(consts_in, 16)

            def bias_row(l, row):
                sp.wait_ge(ln_bias, l * TILES + CR1)
                sp.dma_start(brow[:], orow[bass.ds(row, 1)].rearrange("a n -> (a n)").partition_broadcast(P)).then_inc(brow_in, 16)

            def weights(half, layer, g):
                e = layer * BODIES + g
                n = kept(sp, half * HBODIES + e)
                E = kept(sp, half * STREAM + e)
                wait_apart(sp, split["k"], n + 1)
                sp.wait_ge(split["o"], E + CR1)
                sp.dma_start(raw_ok[:], group(wb, e).rearrange("p c (a n) -> p (c a) n", n=256)).then_inc(raw_in["o"], 16)
                sp.wait_ge(split["q"], E + 1)
                sp.dma_start(raw_vq[:], group(wv, e + 1)).then_inc(raw_in["v"], 16)
                sp.dma_start(raw_vb[:], vrow[bass.ds(e + 1, 1)].rearrange("a b n -> (a b) n").partition_broadcast(P)).then_inc(raw_in["v"], 16)
                sp.wait_ge(split["o"], E + 1 + CR1)
                sp.dma_start(raw_ok[:], group(wk, e + 1)).then_inc(raw_in["k"], 16)
                sp.wait_ge(split["v"], n + 2)
                sp.dma_start(raw_vq[:], group(wa, e + 1)).then_inc(raw_in["q"], 16)

            for half in range(HALVES):
                sp.wait_ge(a_unit, before(half, 0, ALL) + CR1)
                l0_inputs(half)
                if half == 0:
                    sp.dma_start(raw_ok[:], wk[0]).then_inc(raw_in["k"], 16)
                    sp.dma_start(raw_vq[:], wv[0]).then_inc(raw_in["v"], 16)
                    sp.dma_start(raw_vb[:], vrow[0].partition_broadcast(P)).then_inc(raw_in["v"], 16)
                    sp.wait_ge(split["v"], 1)
                    sp.dma_start(raw_vq[:], wa[0]).then_inc(raw_in["q"], 16)
                bias_row(half * NORMS, 0)
                for layer in range(LAYERS):
                    with sp.Fori(0, BODIES - 1) as g:
                        weights(half, layer, g)
                    bias_row(half * NORMS + layer + 1, layer + 1)
                    weights(half, layer, BODIES - 1)
                sp.wait_ge(split["k"], half * HBODIES + HBODIES + 1)
                with sp.Fori(HBODIES, STREAM) as e:
                    sp.wait_ge(split["o"], half * STREAM + e + CR1)
                    sp.dma_start(raw_ok[:], group(wb, e).rearrange("p c (a n) -> p (c a) n", n=256)).then_inc(raw_in["o"], 16)
                    sp.wait_ge(split["q"], half * STREAM + e + 1)
                    sp.dma_start(raw_vq[:], group(wa, e + 1)).then_inc(raw_in["q"], 16)

        @block.gpsimd
        def _(pool):
            pool.sem_inc(split["o"], CR1)
            pool.sem_inc(ln_bias, CR1)
            pool.memset(ident[:], 0.0).then_inc(ident_zero, 1)
            pool.memset(minus_half[:], -0.5).then_inc(ident_zero, 1)
            pool.wait_ge(ident_zero, 2)
            pool.affine_select(out=ident[:], in_=ident[:], compare_op=ALU.not_equal, fill=1.0, base=0,
                               pattern=[[-1, P]], channel_multiplier=1).then_inc(ident_ready, 1)
            pool.wait_ge(bn_step, 1)
            pool.tensor_tensor(bnt[:, 1, :], bnt[:, 0, :], minus_half[:, 0:2], ALU.pow).then_inc(bn_rstd, 1)

            def as_out(raw):
                return raw[:].rearrange("p (c a) n -> p c (a n)", c=2)

            def halve(hi_lo, raw, m, count, hi_count):
                wait_apart(pool, raw_in[m], count)
                pool.tensor_copy(hi_lo[0][:], raw).then_inc(hi_part, 1)
                pool.wait_ge(hi_part, hi_count)
                return pool.tensor_tensor(hi_lo[1][:], raw, f(hi_lo[0][:]), ALU.subtract)

            def halve_v(done, hi_count):
                halve(wvs, raw_vq[:], "v", done * 32, hi_count)
                return pool.tensor_tensor(vb[:], raw_vb[:, 0, :], raw_vb[:, 1, :], ALU.subtract)

            halve(wks, raw_ok[:], "k", 16, 1).then_inc(split["k"], 1)
            halve_v(1, 2).then_inc(split["v"], 1)
            halve(wqs, raw_vq[:], "q", 16, 3).then_inc(split["q"], 1)
            HI0 = 3
            HI_HALF = 4 * HBODIES + 2 * MBODIES

            def rsqrt(l, p):
                pool.wait_ge(ln_eps, l * 2 + p + 1)
                pool.tensor_tensor(rstd[:], vpe[:], minus_half[:], ALU.pow).then_inc(ln_rstd, 1)

            def add_bias(l, p):
                pool.wait_ge(brow_in, l * 16 + 16)
                for t in range(4 * p, 4 * p + 4):
                    pool.wait_ge(ln_z, l * TILES + t + 1)
                    pool.tensor_tensor(x[:, t, :], x[:, t, :], brow[:], ALU.add).then_inc(ln_bias, 1)

            def attention(half, layer, g, kind):
                e = layer * BODIES + g
                n = pool.snap(half * HBODIES + e)
                E = pool.snap(half * STREAM + e)
                hi0 = pool.snap(half * HI_HALF + e * 4 + HI0)
                l = half * NORMS + layer
                units = units_of(kind)
                ub = pool.snap(before(half, e, ALL))
                if kind == FIRST:
                    rsqrt(l, 1)
                pool.wait_ge(a_unit, ub + CR1)
                pool.wait_ge(m_unit, half * (MUNITS * MBODIES) + CR1)
                halve(wos, as_out(raw_ok), "o", E * 16 + 16, hi0 + 1).then_inc(split["o"], 1)
                if kind == FIRST:
                    add_bias(l, 1)
                pool.wait_ge(a_unit, ub + units.index(("k", 1, 1)) + 1 + CR1)
                halve(wks, raw_ok[:], "k", n * 16 + 32, hi0 + 2).then_inc(split["k"], 1)
                pool.wait_ge(a_free, ub + units.index(("v", 1, 1)) + 1 + CR4)
                halve_v(n + 2, hi0 + 3).then_inc(split["v"], 1)
                pool.wait_ge(a_unit, ub + units.index(("q", 1, 1)) + 1 + CR1)
                halve(wqs, raw_vq[:], "q", E * 16 + 32, hi0 + 4).then_inc(split["q"], 1)
                if kind >= LAST:
                    rsqrt(l + 1, 0)
                    add_bias(l + 1, 0)

            def mlp(half, g, first):
                m = pool.snap(half * MBODIES + g)
                E = pool.snap(half * STREAM + g + HBODIES)
                hi0 = pool.snap(half * HI_HALF + g * 2 + HI0 + 4 * HBODIES)
                if first:
                    rsqrt(half * NORMS + LAYERS, 1)
                pool.wait_ge(a_unit, before(half + 1, 0, ALL) + CR1)
                pool.wait_ge(m_unit, m * MUNITS + CR1)
                halve(wos, as_out(raw_ok), "o", E * 16 + 16, hi0 + 1).then_inc(split["o"], 1)
                if first:
                    add_bias(half * NORMS + LAYERS, 1)
                pool.wait_ge(m_unit, m * MUNITS + UNITS_M[first].index(("f", 1, 1)) + 1 + CR1)
                halve(wqs, raw_vq[:], "q", E * 16 + 32, hi0 + 2).then_inc(split["q"], 1)

            with pool.Fori(0, HALVES) as half:
                rsqrt(half * NORMS, 0)
                add_bias(half * NORMS, 0)
                for layer in range(LAYERS):
                    attention(half, layer, 0, FIRST)
                    with pool.Fori(1, BODIES - 1) as g:
                        attention(half, layer, g, MIDDLE)
                    attention(half, layer, BODIES - 1, FINAL if layer == LAYERS - 1 else LAST)
                mlp(half, 0, True)
                with pool.Fori(1, MBODIES) as g:
                    mlp(half, g, False)

        @block.tensor
        def _(pe):
            pe.sem_inc(a_unit, CR1)
            pe.sem_inc(m_unit, CR1)
            pe.sem_inc(a_T, CR2)
            pe.sem_inc(a_pv, CR1)

            def product(o, lhs, rhs, start, stop):
                pe.matmul(o, lhs[0], rhs[0], start=start, stop=False)
                pe.matmul(o, lhs[0], rhs[1], start=False, stop=False)
                return pe.matmul(o, lhs[1], rhs[0], start=False, stop=stop)

            def parts(pr, *ix):
                return tuple(t[(slice(None), *ix)] for t in pr)

            def proj_half(c, w, h, src, p, s):
                for ch in (2 * s, 2 * s + 1):
                    mm = product(bank(c), parts(w, ch, slice(h * P, h * P + P)),
                                 parts(src, ch, slice(p * 512, p * 512 + 512)), ch == 0, ch == CH - 1)
                return mm

            def v_half(c, p, pair_of, s):
                t = p * 512 + (2 * pair_of + s) * P
                for ch in range(CH):
                    mm = product(bank(c)[:, s * 256:s * 256 + 256], parts(cT, ch, slice(t, t + P)),
                                 parts(wvs, ch, slice(0, 256)), ch == 0, ch == CH - 1)
                return mm

            def out_tile(c, p, t):
                for h in range(2):
                    mm = product(bank(c), parts(oT, p, h, slice(t * P, t * P + P)),
                                 parts(wos, h, slice(0, D)), h == 0, h == 1)
                return mm

            def l0_bank_free(half, c):
                if L0[c - RING][0] in TO_V:
                    pe.wait_ge(z_free_v, half * l0_taken(ZUNITS, TO_V) + l0_taken(c - RING, TO_V))
                else:
                    pe.wait_ge(z_free_a, half * l0_taken(ZUNITS, TO_A) + l0_taken(c - RING, TO_A))

            def l0(half):
                pe.wait_ge(m_free, half * (MTILES * MBODIES) + CR4)
                pe.wait_ge(l0_w, half * 64 + 64)
                nv, na = l0_taken(ZUNITS, TO_V), l0_taken(ZUNITS, TO_A)
                for c, (kind, b, part) in enumerate(L0):
                    if kind == "pg" and part == 0:
                        pe.wait_ge(l0_c[b], half * 16 + 16)
                    if kind == "th":
                        pe.wait_ge(l0_x[b], half * 16 + 16)
                    if kind == "cT" and part == 0:
                        pe.wait_ge(l0_c[2 * b + 1], half * 16 + 16)
                    if c >= RING:
                        l0_bank_free(half, c)
                    o = bank(c)
                    if kind == "cT":
                        for t in range(4):
                            mm = pe.transpose(o[:, t * P:t * P + P], c0[:, 4 * b + t, part * P:part * P + P], ident[:])
                    elif kind == "pg":
                        for i in range(2):
                            ch = 2 * part + i
                            for tt in range(2):
                                mm = pe.matmul(o[:, i * 256:i * 256 + 256], c0[:, 2 * b + tt, ch * P:ch * P + P],
                                               wpg[:, tt, :], start=tt == 0, stop=tt == 1)
                    elif kind == "th":
                        for tt in range(2):
                            mm = pe.matmul(o, wth[:, tt, :], x0[:, 2 * b + tt, :], start=tt == 0, stop=tt == 1)
                    elif kind == "M":
                        pe.wait_ge(z_free_v, half * nv + l0_taken(L0.index(("pg", b, 1)), TO_V))
                        for ch in range(CH):
                            mm = pe.matmul(o[:, 0:P], pg[:, ch, P:2 * P], pg[:, ch, 0:P], start=ch == 0, stop=ch == CH - 1)
                    elif kind == "WM":
                        pe.wait_ge(z_free_a, half * na + l0_taken(L0.index(("M", b, 0)), TO_A))
                        mm = pe.matmul(o[:, 0:TOK], msb[:], www_s[:], start=True, stop=True)
                    else:
                        if part == 0:
                            pe.wait_ge(z_free_a, half * na + l0_taken(L0.index(("WM", b, 0)), TO_A))
                        mm = pe.matmul(o, wm[:, part * P:part * P + P], th[:], start=True, stop=True)
                    mm.then_inc(z_unit, 1)

            def prologue(half):
                pe.wait_ge(split["k"], half * HBODIES + 1)
                pe.wait_ge(split["v"], half * HBODIES + 1)
                for c in range(4):
                    pe.wait_ge(ln_affine, half * NORMS * TURNS + c + 1)
                    for s in range(2):
                        mm = proj_half(c, wks, c, cT, 0, s) if c < 2 else v_half(c, 0, c - 2, s)
                    mm.then_inc(pro_unit, 1)

            def norm(l, p, units, bank_free):
                pe.wait_ge(ln_z, l * TILES + 4 * p + 4)
                for ch, c in enumerate(units):
                    bank_free(c)
                    for t in range(4):
                        mm = pe.transpose(bank(c)[:, t * P:t * P + P], z[:, t, ch * P:ch * P + P], ident[:])
                    mm.then_inc(ln_T, 1)

            def attention(half, layer, g, kind):
                e = layer * BODIES + g
                n = half * HBODIES + e
                units = units_of(kind)
                ub = pe.snap(before(half, e, ALL))
                jb = pe.snap(n * ITEMS)
                E = pe.snap(half * STREAM + e)
                l = half * NORMS + layer

                def bank_free(c):
                    pe.wait_ge(a_free, ub + c - RING + 1 + CR4)

                def unit(c, s, turned):
                    what, p, i = units[c]
                    if s == 0 or what == "w":
                        bank_free(c)
                        if kind == FIRST and c < RING:
                            pe.wait_ge(pro_free, half * 4 + c + 1)
                        if turned is not None:
                            pe.wait_ge(ln_affine, turned)
                    if c == 0 and s == 0:
                        pe.wait_ge(split["q"], E + 1)
                        if kind == FIRST:
                            pe.wait_ge(ln_h, l * TURNS + CH + CR2)
                    if (what, p, i, s, kind) == ("q", 1, 0, 0, FIRST):
                        pe.wait_ge(ln_h, l * TURNS + TURNS + CR2)
                    if (what, i, s) == ("K", 0, 0):
                        pe.wait_ge(split["k"], n + 2)
                    if (what, i, s) == ("V", 0, 0):
                        pe.wait_ge(split["v"], n + 2)
                    if what == "q":
                        mm = proj_half(c, wqs, i, hT, p, s)
                    elif what in "kK":
                        mm = proj_half(c, wks, i, cT, p, s)
                    elif what in "vV":
                        mm = v_half(c, p, i, s)
                    else:
                        if (p, i) == (0, 0):
                            pe.wait_ge(split["o"], E + 1 + CR1)
                        if i in (0, 2):
                            pe.wait_ge(a_o, jb + 4 * p + (3 if i == 0 else 4) + CR1)
                        mm = out_tile(c, p, i)
                    if s == 1:
                        mm.then_inc(a_unit, 1)

                def logits(j):
                    p, h, b = item(j)
                    if b == 0:
                        pe.wait_ge(a_free, ub + units.index(("q", p, h)) + 1 + CR4)
                    pe.wait_ge(a_exp, jb + j + CR1)
                    for qt in range(2):
                        q0 = b * 256 + qt * P
                        mm = product(S[:, qt, 0:258], parts(qT, h, slice(q0, q0 + P)), parts(kT, p, h, b), True, True)
                    mm.then_inc(a_logit, 1)

                def turn(j):
                    pe.wait_ge(a_prob, jb + j + 1)
                    pe.wait_ge(a_pt, jb + j + CR1)
                    for tt in range(2):
                        for qt in range(2):
                            mm = pe.transpose(T[:, tt, qt * P:qt * P + P],
                                              probs[:, j % 2, qt, tt * P:tt * P + P], ident[:])
                    mm.then_inc(a_T, 1)

                def values(j):
                    p, h, b = item(j)
                    pe.wait_ge(a_pt, jb + j + 1 + CR1)
                    pe.wait_ge(a_o, jb + j + CR1)
                    for tt in range(2):
                        mm = product(O[:, 0:256], parts(v, p, 2 * b + tt, slice(h * P, h * P + P)),
                                     parts(PT, tt), tt == 0, tt == 1)
                    mm.then_inc(a_pv, 1)

                turned = {}
                for what, *a in steps(kind):
                    if what == "U":
                        unit(*a, turned.get(a[0]))
                    elif what == "L":
                        logits(*a)
                    elif what == "T":
                        turn(*a)
                    elif what == "P":
                        values(*a)
                    elif what == "Z":
                        p, ln, nxt = a[0], l if kind == FIRST else l + 1, norm_units(kind)
                        norm(ln, p, nxt, bank_free)
                        turned = {c: ln * TURNS + CH * p + ch + 1 for ch, c in enumerate(nxt)}

            def mlp(half, g, first):
                m = half * MBODIES + g
                E = pe.snap(half * STREAM + g + HBODIES)
                units = UNITS_M[first]
                l = half * NORMS + LAYERS

                def bank_free(c):
                    if c < RING and first:
                        pe.wait_ge(a_free, before(half + 1, 0, ALL) + c - RING + 1 + CR4)
                    elif c < RING:
                        pe.wait_ge(m_free, m * MTILES + c - RING + 1 + CR4)
                    elif units[c - RING][0] == "f":
                        pe.wait_ge(m_gelu, m * 4 + nth(units, c - RING, "f"))
                    else:
                        pe.wait_ge(m_free, m * MTILES + nth(units, c - RING, "w") + CR4)

                pe.wait_ge(split["q"], E + 1)
                for c, (what, p, i) in enumerate(units):
                    if first and c == 2:
                        norm(l, 1, range(2, 6), bank_free)
                    bank_free(c)
                    if first and c in range(2, 6):
                        pe.wait_ge(ln_affine, l * TURNS + CH + c - 2 + 1)
                    if what == "f":
                        if first:
                            pe.wait_ge(ln_h, l * TURNS + CH * p + CH + CR2)
                        for s in range(2):
                            mm = proj_half(c, wqs, i, hT, p, s)
                        mm.then_inc(m_unit, 1)
                    else:
                        if (p, i) == (0, 0):
                            pe.wait_ge(split["o"], E + 1 + CR1)
                        if i == 0:
                            pe.wait_ge(m_act, m * 4 + 2 * p + 2 + CR2)
                        out_tile(c, p, i).then_inc(m_unit, 1)

            pe.wait_ge(ident_ready, 1)
            with pe.Fori(0, HALVES) as half:
                l0(half)
                norm(half * NORMS, 0, range(ZUNITS, ZUNITS + RING), lambda c: l0_bank_free(half, c))
                prologue(half)
                for layer in range(LAYERS):
                    attention(half, layer, 0, FIRST)
                    with pe.Fori(1, BODIES - 1) as g:
                        attention(half, layer, g, MIDDLE)
                    attention(half, layer, BODIES - 1, FINAL if layer == LAYERS - 1 else LAST)
                mlp(half, 0, True)
                with pe.Fori(1, MBODIES) as g:
                    mlp(half, g, False)

        @block.scalar
        def _(act):
            act.sem_inc(a_exp, CR1)
            act.sem_inc(stored, CR1)
            act.wait_ge(consts_in, 16 * 5)
            act.activation(bkx[0][:], hc[:, 2, :], ACT.Copy).then_inc(bk_hi, 1)

            def l0(half):
                for c, (kind, b, part) in enumerate(L0):
                    o = bank(c)
                    if kind == "pg":
                        continue
                    act.wait_ge(z_unit, half * ZUNITS + c + 1)
                    if kind == "cT":
                        act.activation(cT[0][:, part, b * 512:b * 512 + 512], o, ACT.Copy).then_inc(z_hi, 1)
                    elif kind == "th":
                        act.activation(th[:], o, ACT.Identity, bias=thb_s[:, 0:1]).then_inc(z_free_a, 1)
                    elif kind == "M":
                        act.activation(msb[:], o[:, 0:P], ACT.Copy, scale=1.0 / D).then_inc(z_free_a, 1)
                    elif kind == "WM":
                        act.activation(wm[:], o[:, 0:TOK], ACT.Copy).then_inc(z_free_a, 1)
                    else:
                        k = 2 * b + part
                        if k == 0:
                            act.wait_ge(bn_ready, 1)
                        act.wait_ge(z_x, half * TILES + k - 1 + CR2)
                        act.activation(tmp[:, part, :], o, ACT.Identity, bias=bns[:, 1, part:part + 1],
                                       scale=bns[:, 0, part:part + 1]).then_inc(z_free_a, 1)

            def kv_hi(c, p, h, waits, b, count, hi, v32, col):
                if h < 2:
                    act.wait_ge(waits, count)
                    act.activation(kview(0, p, h), two(bank(c)), ACT.Identity, bias=col).then_inc(hi, 1)
                else:
                    act.wait_ge(v32, b)
                    act.activation(vview(0, p, h - 2), two(tmp[:, h - 2, :]), ACT.Copy).then_inc(hi, 1)

            def norm(l, li, p, ch, c):
                k = CH * p + ch
                wait_apart(act, ln_T, l * TURNS + k + 1)
                wait_apart(act, ln_h, l * TURNS + k - 1 + CR2)
                act.activation(aff[:, k % 2, :], bank(c), ACT.Identity, bias=lnc[:, 1, li * CH + ch:li * CH + ch + 1],
                               scale=lnc[:, 0, li * CH + ch:li * CH + ch + 1]).then_inc(ln_affine, 1)
                act.wait_ge(ln_affine, l * TURNS + k + 1)
                act.activation(hT[0][:, ch, p * 512:p * 512 + 512], aff[:, k % 2, :], ACT.Copy).then_inc(ln_hi, 1)

            def attention(half, layer, g, kind):
                e = layer * BODIES + g
                n = half * HBODIES + e
                units = units_of(kind)
                ub = act.snap(before(half, e, ALL))
                jb = act.snap(n * ITEMS)
                vu = act.snap(before(half, e, VS))
                head = kept(act, e * 2)

                def unit_hi(c):
                    what, p, i = units[c]
                    if what == "q":
                        wait_apart(act, a_unit, ub + c + 1 + CR1)
                        act.activation(qslot(0, i), bank(c), ACT.Identity,
                                       bias=hc[:, 0, bass.ds(head + i, 1)]).then_inc(a_hi, 1)
                    elif what in "kK":
                        wait_apart(act, a_unit, ub + c + 1 + CR1)
                        act.activation(kview(0, p, i), two(bank(c)), ACT.Identity,
                                       bias=hc[:, 1, bass.ds(head + i + 2 * (what == "K"), 1)]).then_inc(a_hi, 1)
                    elif what in "vV":
                        act.wait_ge(a_v32, vu + nth(units, c, VS))
                        act.activation(vview(0, p, i), two(tmp[:, i, :]), ACT.Copy).then_inc(a_hi, 1)

                def softmax(j):
                    act.wait_ge(a_max, jb + j + 1)
                    act.wait_ge(a_T, jb + j - 1 + CR2)
                    for qt in range(2):
                        ins = act.activation(probs[:, j % 2, qt, 0:257], S[:, qt, 0:257], ACT.Exp,
                                             bias=nm[:, j % 2, qt:qt + 1], scale=SCALE,
                                             accum_out=sums[:, j % 2, qt:qt + 1])
                    ins.then_inc(a_exp, 1)

                def turned_hi(j):
                    act.wait_ge(a_T, jb + j + 1 + CR2)
                    act.wait_ge(a_pv, jb + j + CR1)
                    act.activation(PT[0][:], T[:], ACT.Copy).then_inc(a_pthi, 1)

                def o_hi(j):
                    p, h, b = item(j)
                    wait_apart(act, a_pv, jb + j + 1 + CR1)
                    act.activation(oT[0][:, p, h, b * 256:b * 256 + 256], O[:, 0:256], ACT.Identity,
                                   bias=hc[:, 3, bass.ds(head + h, 1)]).then_inc(a_ohi, 1)

                for what, *a in steps(kind):
                    if what == "U":
                        if a[1] == 1:
                            unit_hi(a[0])
                    elif what == "L":
                        if a[0] == 0:
                            softmax(0)
                    elif what == "T":
                        turned_hi(*a)
                        if a[0] + 1 < ITEMS:
                            softmax(a[0] + 1)
                    elif what == "P":
                        o_hi(*a)
                    elif what == "A":
                        nxt = layer if kind == FIRST else layer + 1
                        norm(half * NORMS + nxt, nxt, *a, norm_units(kind)[a[1]])

            def mlp(half, g, first):
                m = half * MBODIES + g
                done = 0
                for c, (what, p, i) in enumerate(UNITS_M[first]):
                    if first and c == 2:
                        for ch in range(CH):
                            norm(half * NORMS + LAYERS, LAYERS, 1, ch, 2 + ch)
                    if what == "f":
                        wait_apart(act, m_unit, m * MUNITS + c + 1 + CR1)
                        wait_apart(act, m_act, m * 4 + done - 1 + CR2)
                        act.activation(tmp[:, i, :], bank(c), ACT.Gelu,
                                       bias=f1c[:, bass.ds(g * 2 + i, 1)]).then_inc(m_gelu, 1)
                        done += 1

            with act.Fori(0, HALVES) as half:
                l0(half)
                for ch in range(CH):
                    norm(half * NORMS, 0, 0, ch, ch)
                act.wait_ge(z_x, half * TILES + TILES + CR2)
                for c in range(4):
                    kv_hi(c, 0, c, pro_unit, half * 2 + c - 1, half * 4 + c + 1, pro_hi, pro_v32, hc[:, 1, c % 2:c % 2 + 1])
                for layer in range(LAYERS):
                    attention(half, layer, 0, FIRST)
                    with act.Fori(1, BODIES - 1) as g:
                        attention(half, layer, g, MIDDLE)
                    attention(half, layer, BODIES - 1, FINAL if layer == LAYERS - 1 else LAST)
                mlp(half, 0, True)
                with act.Fori(1, MBODIES) as g:
                    mlp(half, g, False)
                act.wait_ge(m_free, half * (MTILES * MBODIES) + MTILES * MBODIES + CR4)
                for p in range(2):
                    act.dma_start(out[bass.ds(half * 2 + p, 1)].rearrange("a t p n -> p (a t) n"),
                                  x[:, 4 * p:4 * p + 4, :]).then_inc(stored, 16)
            act.wait_ge(stored, HALVES * 32 + CR1)

        @block.vector
        def _(dve):
            for s, k in ((m_free, CR4), (a_free, CR4), (z_x, CR2), (ln_h, CR2), (a_pt, CR1), (a_o, CR1), (m_act, CR2)):
                dve.sem_inc(s, k)
            dve.wait_ge(consts_in, 16 * 5)
            dve.tensor_scalar(bnt[:, 0, :], bnc[:, 3, :], EPS, None, ALU.add).then_inc(bn_step, 1)
            dve.wait_ge(bn_rstd, 1)
            dve.tensor_tensor(bns[:, 0, :], bnc[:, 0, :], bnt[:, 1, :], ALU.mult).then_inc(bn_step, 1)
            dve.tensor_tensor(bnt[:, 2, :], bnc[:, 4, :], bnc[:, 2, :], ALU.subtract).then_inc(bn_step, 1)
            dve.wait_ge(bn_step, 3)
            dve.tensor_tensor(bnt[:, 2, :], bnt[:, 2, :], bns[:, 0, :], ALU.mult).then_inc(bn_step, 1)
            dve.wait_ge(bn_step, 4)
            dve.tensor_tensor(bns[:, 1, :], bnt[:, 2, :], bnc[:, 1, :], ALU.add).then_inc(bn_ready, 1)
            dve.wait_ge(bk_hi, 1)
            dve.tensor_tensor(bkx[1][:], hc[:, 2, :], f(bkx[0][:]), ALU.subtract).then_inc(bk_lo, 1)
            dve.wait_ge(bk_lo, 1)

            def tile_stats(t):
                dve.bn_stats(stats[:, t % 4, :], x[:, t, :]).then_inc(ln_stats, 1)

            def moments(l, p):
                for t in range(4):
                    wait_apart(dve, ln_stats, l * TILES + 4 * p + t + 1)
                    dve.bn_aggr(mv[:, t, :], stats[:, t, :]).then_inc(ln_mv, 1)
                dve.wait_ge(ln_mv, l * TILES + 4 * p + 4)
                dve.tensor_scalar(vpe[:], mv[:, :, 1], EPS, None, ALU.add).then_inc(ln_eps, 1)

            def normalise(l, p):
                dve.wait_ge(ln_rstd, l * 2 + p + 1)
                for t in range(4):
                    dve.tensor_scalar(z[:, t, :], x[:, 4 * p + t, :], mv[:, t, 0:1], rstd[:, t:t + 1],
                                      ALU.subtract, ALU.mult).then_inc(ln_z, 1)

            def l0(half):
                his = 0
                for c, (kind, b, part) in enumerate(L0):
                    o = bank(c)
                    if kind == "cT":
                        his += 1
                        dve.wait_ge(z_hi, half * 2 * CH + his)
                        to = slice(b * 512, b * 512 + 512)
                        dve.tensor_tensor(cT[1][:, part, to], o, f(cT[0][:, part, to]), ALU.subtract).then_inc(z_free_v, 1)
                        if his == 2 * CH - 1:
                            normalise(half * NORMS, 0)
                    elif kind == "pg":
                        dve.wait_ge(z_unit, half * ZUNITS + c + 1)
                        dve.tensor_tensor(pg[:, 2 * part:2 * part + 2, :], two(o),
                                          pgb_s[:].unsqueeze(1).to_broadcast([P, 2, 256]), ALU.add).then_inc(z_free_v, 1)
                    elif kind == "wy":
                        k = 2 * b + part
                        if k == 0:
                            dve.wait_ge(stored, half * 32 + CR1)
                        dve.wait_ge(z_free_a, half * l0_taken(ZUNITS, TO_A) + l0_taken(c, TO_A))
                        dve.tensor_tensor(x[:, k, :], tmp[:, part, :], x0[:, k, :], ALU.add).then_inc(z_x, 1)
                        dve.wait_ge(z_x, half * TILES + k + 1 + CR2)
                        tile_stats(k)
                        if k == 3:
                            moments(half * NORMS, 0)

            def k_lo(c, p, h, hi, hi_count, col, bk_col):
                for part in range(2):
                    dve.tensor_copy(kT[part][:, p, h, :, 256:258],
                                    bk_col(f(bkx[part][:])).unsqueeze(2).to_broadcast([P, 2, 2]))
                dve.wait_ge(hi, hi_count)
                return dve.scalar_tensor_tensor(out=kview(1, p, h), in0=two(bank(c)), scalar=col,
                                                in1=f(kview(0, p, h)), op0=ALU.add, op1=ALU.subtract)

            def v_lo(c, p, i, v32, v_count, hi, hi_count):
                dve.tensor_tensor(two(tmp[:, i, :]), two(bank(c)), vb[:].unsqueeze(1).to_broadcast([P, 2, 256]),
                                  ALU.add).then_inc(v32, 1)
                dve.wait_ge(v32, v_count)
                dve.wait_ge(hi, hi_count)
                return dve.tensor_tensor(vview(1, p, i), two(tmp[:, i, :]), f(vview(0, p, i)), ALU.subtract)

            def prologue(half):
                dve.wait_ge(z_x, half * TILES + TILES + CR2)
                for c in range(4):
                    dve.wait_ge(pro_unit, half * 4 + c + 1)
                    if c < 2:
                        ins = k_lo(c, 0, c, pro_hi, half * 4 + c + 1, hc[:, 1, c:c + 1], lambda t, c=c: t[:, c:c + 1])
                    else:
                        ins = v_lo(c, 0, c - 2, pro_v32, half * 2 + c - 1, pro_hi, half * 4 + c + 1)
                    ins.then_inc(pro_free, 1)

            def norm_lo(l, p, ch):
                k = p * CH + ch
                to = slice(p * 512, p * 512 + 512)
                dve.wait_ge(ln_hi, l * TURNS + k + 1)
                dve.tensor_tensor(hT[1][:, ch, to], aff[:, k % 2, :], f(hT[0][:, ch, to]), ALU.subtract).then_inc(ln_h, 1)

            def attention(half, layer, g, kind):
                e = layer * BODIES + g
                n = half * HBODIES + e
                units = units_of(kind)
                ub = dve.snap(before(half, e, ALL))
                jb = dve.snap(n * ITEMS)
                hb = dve.snap(before(half, e, OPERANDS))
                vu = dve.snap(before(half, e, VS))
                head = kept(dve, e * 2)
                l = half * NORMS + layer

                def unit_lo(c):
                    what, p, i = units[c]
                    hi_count = hb + nth(units, c, OPERANDS)
                    if what == "q":
                        dve.wait_ge(a_hi, hi_count)
                        ins = dve.scalar_tensor_tensor(out=qslot(1, i), in0=bank(c), scalar=hc[:, 0, bass.ds(head + i, 1)],
                                                       in1=f(qslot(0, i)), op0=ALU.add, op1=ALU.subtract)
                    elif what in "kK":
                        at = head + i + 2 * (what == "K")
                        dve.wait_ge(a_unit, ub + c + 1 + CR1)
                        ins = k_lo(c, p, i, a_hi, hi_count, hc[:, 1, bass.ds(at, 1)], lambda t: t[:, bass.ds(at, 1)])
                    elif what in "vV":
                        if i == 0:
                            dve.wait_ge(split["v"], n + 1 + (what == "V"))
                        dve.wait_ge(a_unit, ub + c + 1 + CR1)
                        ins = v_lo(c, p, i, a_v32, vu + nth(units, c, VS), a_hi, hi_count)
                    else:
                        if kind == FIRST and i == 0:
                            dve.wait_ge(ln_bias, l * TILES + 4 * p + 4 + CR1)
                        t = 4 * p + i
                        dve.wait_ge(a_unit, ub + c + 1 + CR1)
                        ins = dve.tensor_tensor(x[:, t, :], x[:, t, :], bank(c), ALU.add)
                    ins.then_inc(a_free, 1)

                def stats_of(c):
                    dve.wait_ge(a_free, ub + c + 1 + CR4)
                    tile_stats(4 * units[c][1] + units[c][2])

                def max_of(j):
                    dve.wait_ge(a_logit, jb + j + 1)
                    dve.tensor_reduce(mx[:, j % 2, :], S[:, :, 0:257], AX.X, ALU.max).then_inc(a_rawmax, 1)
                    dve.wait_ge(a_rawmax, jb + j + 1)
                    dve.tensor_scalar(nm[:, j % 2, :], mx[:, j % 2, :], -SCALE, None, ALU.mult).then_inc(a_max, 1)

                def divide(j):
                    r = j % 2
                    dve.wait_ge(a_exp, jb + j + 1 + CR1)
                    dve.reciprocal(rs[:, r, :], sums[:, r, :]).then_inc(a_rcp, 1)
                    dve.wait_ge(a_rcp, jb + j + 1)
                    for qt in range(2):
                        ins = dve.tensor_scalar(probs[:, r, qt, 0:256], probs[:, r, qt, 0:256], rs[:, r, qt:qt + 1], None, ALU.mult)
                    ins.then_inc(a_prob, 1)

                def turned_lo(j):
                    dve.wait_ge(a_pthi, jb + j + 1)
                    dve.tensor_tensor(PT[1][:], T[:], f(PT[0][:]), ALU.subtract).then_inc(a_pt, 1)

                def o_lo(j):
                    p, h, b = item(j)
                    to = slice(b * 256, b * 256 + 256)
                    dve.wait_ge(a_ohi, jb + j + 1)
                    dve.scalar_tensor_tensor(out=oT[1][:, p, h, to], in0=O[:, 0:256], scalar=hc[:, 3, bass.ds(head + h, 1)],
                                             in1=f(oT[0][:, p, h, to]), op0=ALU.add, op1=ALU.subtract).then_inc(a_o, 1)

                if kind == FIRST:
                    dve.wait_ge(z_x, half * TILES + TILES + CR2)
                    dve.wait_ge(a_free, ub + CR4)
                    moments(l, 1)
                for what, *a in steps(kind):
                    if what == "U":
                        c, s = a
                        if s == 0 or units[c] == ("w", 1, 0):
                            continue
                        unit_lo(c)
                        if kind == FIRST and c == 0:
                            normalise(l, 1)
                        if kind >= LAST and units[c] in [("w", 0, t) for t in range(3)]:
                            stats_of(c)
                        if kind >= LAST and units[c] == ("w", 1, 3):
                            for t in range(4):
                                stats_of(units.index(("w", 1, t)))
                    elif what == "L":
                        max_of(*a)
                        if a[0] == 0:
                            divide(0)
                    elif what == "T":
                        turned_lo(*a)
                        if a[0] + 1 < ITEMS:
                            divide(a[0] + 1)
                        if kind >= LAST and a[0] == ITEMS - 3:
                            stats_of(units.index(("w", 0, 3)))
                            moments(l + 1, 0)
                    elif what == "P":
                        o_lo(*a)
                        if a[0] == ITEMS - 1:
                            unit_lo(units.index(("w", 1, 0)))
                        if kind >= LAST and a[0] == ITEMS - 3:
                            normalise(l + 1, 0)
                    elif what == "A":
                        norm_lo(l if kind == FIRST else l + 1, *a)

            def mlp(half, g, first):
                m = half * MBODIES + g
                l = half * NORMS + LAYERS
                done = 0
                if first:
                    dve.wait_ge(a_free, before(half + 1, 0, ALL) + CR4)
                    moments(l, 1)
                    normalise(l, 1)
                for c, (what, p, i) in enumerate(UNITS_M[first]):
                    if first and c == 2:
                        for ch in range(CH):
                            norm_lo(l, 1, ch)
                    if what == "f":
                        done += 1
                        dve.wait_ge(m_gelu, m * 4 + done)
                        dve.tensor_copy(oT[0][:, p, i, :], tmp[:, i, :]).then_inc(m_hi, 1)
                        dve.wait_ge(m_hi, m * 4 + done)
                        dve.tensor_tensor(oT[1][:, p, i, :], tmp[:, i, :], f(oT[0][:, p, i, :]), ALU.subtract).then_inc(m_act, 1)
                    else:
                        if first and i == 0:
                            dve.wait_ge(ln_bias, l * TILES + 4 * p + 4 + CR1)
                        t = 4 * p + i
                        dve.wait_ge(m_unit, m * MUNITS + c + 1 + CR1)
                        dve.tensor_tensor(x[:, t, :], x[:, t, :], bank(c), ALU.add).then_inc(m_free, 1)

            with dve.Fori(0, HALVES) as half:
                l0(half)
                for ch in range(CH):
                    norm_lo(half * NORMS, 0, ch)
                prologue(half)
                for layer in range(LAYERS):
                    attention(half, layer, 0, FIRST)
                    with dve.Fori(1, BODIES - 1) as g:
                        attention(half, layer, g, MIDDLE)
                    attention(half, layer, BODIES - 1, FINAL if layer == LAYERS - 1 else LAST)
                mlp(half, 0, True)
                with dve.Fori(1, MBODIES) as g:
                    mlp(half, g, False)


def _laid_out(i):
    a = {k.replace("L0_xattn_", "").replace("L1_xattn_", "L1"): np.ascontiguousarray(v) for k, v in i.items()}

    def col(vec):
        return vec.reshape(-1, P).T

    def heads(*vecs):
        c = col(np.concatenate([v.reshape(-1) for v in vecs]))
        return np.concatenate([c, c[:, :2]], 1)

    def in_groups(w):
        return w.reshape(CH, P, -1, 256).transpose(2, 1, 0, 3)

    def out_groups(w):
        return w.reshape(-1, 2, P, D).transpose(0, 2, 1, 3)

    def both(name):
        return [a[f"L1{name}1"], a[f"L1{name}2"]]

    q = np.concatenate([in_groups(w) for w in both("wq")] + [in_groups(a["L1w_fc1"])])
    k, v = (np.concatenate([in_groups(w) for w in both(s)]) for s in ("wk", "wv"))
    vr = np.stack([np.concatenate([r.reshape(-1) for r in both(s)]).reshape(HBODIES, 256) for s in ("bv", "bias_v")], 1)
    tiles = (HALVES * 2, 4, P, D)
    lns = [[a[f"L1ln{n}_{s}"] for n in ("1", "2", "_mlp")] for s in ("scale", "offset")]
    return {
        "x_in": a["x"].reshape(tiles),
        "ctx_in": a["ctx_2048"].reshape(tiles),
        "thw": a["theta_w"].T.reshape(2, P, CI).transpose(1, 0, 2),
        "thb": col(a["theta_b"]),
        "pgw": np.concatenate([a["phi_w"].T, a["g_w"].T], 1).reshape(2, P, 2 * CI).transpose(1, 0, 2),
        "pgb": np.concatenate([a["phi_b"], a["g_b"]]),
        "www": a["w_w"].T,
        "bncol": np.stack([col(a[s]) for s in ("bn_gamma", "bn_beta", "bn_mean", "bn_var", "w_b")], 1),
        "wa": np.concatenate([q, q[:1]]),
        "wk": np.concatenate([k, k[:1]]),
        "wv": np.concatenate([v, v[:1]]),
        "wb": np.concatenate([out_groups(w) for w in both("wo")] + [out_groups(a["L1w_fc2"])]),
        "hcol": np.stack([heads(*both(s)) for s in ("bq", "bk", "bias_k", "bias_v")], 1),
        "vrow": np.concatenate([vr, vr[:1]]),
        "lncol": np.stack([np.concatenate([col(x) for x in r], 1) for r in lns], 1),
        "f1col": col(a["L1b_fc1"]),
        "orow": np.stack([*both("bo"), a["L1b_fc2"]]),
    }


def kernel(**inputs):
    import concourse.bacc as bacc
    from concourse.bass_utils import run_bass_kernel_spmd

    nc = bacc.Bacc("TRN2", target_bir_lowering=False, num_devices=1)
    arrays = {k: np.ascontiguousarray(v) for k, v in _laid_out(inputs).items()}
    args = [nc.dram_tensor(k, v.shape, mybir.dt.from_np(v.dtype), kind="ExternalInput").ap() for k, v in arrays.items()]
    out = nc.dram_tensor("out", (HALVES * 2, 4, P, D), F32, kind="ExternalOutput").ap()
    bass_xattn(nc, *args, out)
    r = run_bass_kernel_spmd(nc, [arrays], core_ids=[0])
    return r.results[0]["out"].reshape(B, TOK, D)
```
